# Optimizing a Trainium2 kernel written in Bass

```python
import numpy as np
import jax
import jax.numpy as jnp

def _softmax(x, axis=-1):
    return jax.nn.softmax(x, axis=axis)

def _gelu(x):
    return jax.nn.gelu(x, approximate=True)

def _silu(x):
    return jax.nn.silu(x)

def _sigmoid(x):
    return jax.nn.sigmoid(x)

def _layernorm(x, axis=-1, eps=1e-05):
    m = jnp.mean(x, axis=axis, keepdims=True)
    v = jnp.var(x, axis=axis, keepdims=True)
    return (x - m) / jnp.sqrt(v + eps)

def _scatter_add(tgt, idx, src, axis=0):
    return tgt.at[idx].add(src)

def _segment_sum(src, seg, n):
    return jax.ops.segment_sum(src, seg, n)
kernel_name = 'mk_adj_resnorm_d2_adj_r2_2d7a57'

def setup_inputs(seed: int=0):
    np.random.seed(seed)
    _w = jnp.asarray

    def _rec_inputs():
        import jax
        import jax.numpy as jnp
        _gk = jax.random.key(seed)
        x = -9.229e-05 + 0.9999 * jax.random.normal(jax.random.fold_in(_gk, 1), (128, 64, 512), jnp.float32)
        _a = jax.random.bernoulli(jax.random.fold_in(_gk, 2), 0.125, (64, 64))
        _a = jnp.logical_or(_a, jnp.swapaxes(_a, -1, -2))
        _a = jnp.logical_or(_a, jnp.eye(64, dtype=bool))
        _af = _a.astype(jnp.float32)
        adj = _af
        return (x, adj)
    x, adj = _rec_inputs()

    def _L0_gnn_setup():
        import jax, jax.numpy as jnp
        import numpy as np
        DIM = 199
        K_HOP = 3

        def _khop_support(n, k):
            A = np.eye(n, dtype=np.float64)
            idx = np.arange(n)
            A[idx, (idx + 1) % n] = 1.0
            A[(idx + 1) % n, idx] = 1.0
            S = np.linalg.matrix_power(A, k)
            return (S > 0).astype(np.float32)
        key = jax.random.key(seed)
        kx, kk = jax.random.split(key)
        batch, n, f = (128, DIM, 512)
        x = jax.random.normal(kx, (batch, n, f), dtype=jnp.float32)
        support = jnp.asarray(_khop_support(n, K_HOP))
        limit = float(np.sqrt(6.0 / (n + n)))
        kernel = jax.random.uniform(kk, (n, n), minval=-limit, maxval=limit, dtype=jnp.float32)
        bias = jnp.zeros((f,), dtype=jnp.float32)
        return {'x': x, 'support': support, 'kernel': kernel, 'bias': bias}
    _L0_gnn_all = _L0_gnn_setup()
    _L0_gnn_in = {k: v for k, v in _L0_gnn_all.items() if k in ('bias',)}
    del _L0_gnn_all

    def _L1_gnn_setup():
        import jax, jax.numpy as jnp
        import numpy as np
        EPS = 1e-08

        def _row_stochastic_causal(A, causal_mask):
            A = A * causal_mask
            deg = jnp.maximum(A.sum(axis=-1, keepdims=True), EPS)
            return A / deg
        key = jax.random.key(seed)
        k = jax.random.split(key, 5)
        B, N, D = (4, 1024, 512)
        s = 1.0 / np.sqrt(D)
        h = jax.random.normal(k[0], (B, N, D), dtype=jnp.float32)
        W_lang = jax.random.normal(k[1], (D, D), dtype=jnp.float32) * s
        W_grav = jax.random.normal(k[2], (D, D), dtype=jnp.float32) * s
        W_V = jax.random.normal(k[3], (D, D), dtype=jnp.float32) * s
        W_O = jax.random.normal(k[4], (D, D), dtype=jnp.float32) * s
        causal_mask = jnp.tril(jnp.ones((N, N), dtype=jnp.float32))
        gate_logit = jnp.zeros((), jnp.float32)
        log_sigma = jnp.zeros((), jnp.float32)
        return {'h': h, 'causal_mask': causal_mask, 'W_lang': W_lang, 'W_grav': W_grav, 'W_V': W_V, 'W_O': W_O, 'gate_logit': gate_logit, 'log_sigma': log_sigma}
    _L1_gnn_all = _L1_gnn_setup()
    _L1_gnn_in = {k: v for k, v in _L1_gnn_all.items() if k in ('W_lang', 'W_grav', 'W_V', 'W_O', 'gate_logit', 'log_sigma')}
    del _L1_gnn_all
    return {'x': x, 'adj': adj, 'L0_gnn_bias': _L0_gnn_in['bias'], 'L1_gnn_W_lang': _L1_gnn_in['W_lang'], 'L1_gnn_W_grav': _L1_gnn_in['W_grav'], 'L1_gnn_W_V': _L1_gnn_in['W_V'], 'L1_gnn_W_O': _L1_gnn_in['W_O'], 'L1_gnn_gate_logit': _L1_gnn_in['gate_logit'], 'L1_gnn_log_sigma': _L1_gnn_in['log_sigma']}

def reference(x, adj, L0_gnn_bias, L1_gnn_W_lang, L1_gnn_W_grav, L1_gnn_W_V, L1_gnn_W_O, L1_gnn_gate_logit, L1_gnn_log_sigma):
    import jax
    import jax.numpy as jnp

    def _L0_gnn_ref(x, support, kernel, bias):
        import jax, jax.numpy as jnp
        import numpy as np
        DIM = 199
        K_HOP = 3

        def _khop_support(n, k):
            A = np.eye(n, dtype=np.float64)
            idx = np.arange(n)
            A[idx, (idx + 1) % n] = 1.0
            A[(idx + 1) % n, idx] = 1.0
            S = np.linalg.matrix_power(A, k)
            return (S > 0).astype(np.float32)
        W = support * kernel
        out = jnp.einsum('bnf,nm->bmf', x, W)
        out = out + bias
        return out

    def _L1_gnn_ref(h, causal_mask, W_lang, W_grav, W_V, W_O, gate_logit, log_sigma):
        import jax, jax.numpy as jnp
        import numpy as np
        EPS = 1e-08

        def _row_stochastic_causal(A, causal_mask):
            A = A * causal_mask
            deg = jnp.maximum(A.sum(axis=-1, keepdims=True), EPS)
            return A / deg
        z_l = jnp.einsum('bnd,ed->bne', h, W_lang)
        z_g = jnp.einsum('bnd,ed->bne', h, W_grav)
        v = jnp.einsum('bnd,ed->bne', h, W_V)
        N = h.shape[-2]
        not_eye = 1.0 - jnp.eye(N, dtype=h.dtype)
        zn = z_l / jnp.maximum(jnp.linalg.norm(z_l, axis=-1, keepdims=True), EPS)
        A_l = jnp.maximum(jnp.einsum('bnd,bmd->bnm', zn, zn), 0.0) * not_eye
        sq = jnp.sum(z_g * z_g, axis=-1, keepdims=True)
        d2 = jnp.maximum(sq + jnp.swapaxes(sq, -1, -2) - 2.0 * jnp.einsum('bnd,bmd->bnm', z_g, z_g), 0.0)
        sigma = jnp.exp(log_sigma)
        A_g = jnp.exp(-d2 / (2.0 * sigma * sigma)) * not_eye
        K_l = _row_stochastic_causal(A_l, causal_mask)
        K_g = _row_stochastic_causal(A_g, causal_mask)
        w_l = jax.nn.sigmoid(gate_logit)
        K = w_l * K_l + (1.0 - w_l) * K_g
        out = jnp.einsum('bnm,bmd->bnd', K, v)
        return jnp.einsum('bnd,ed->bne', out, W_O)
    x = _layernorm(x + _L0_gnn_ref(x, adj, adj, L0_gnn_bias), axis=-1)
    x = _layernorm(x + _L1_gnn_ref(x, adj, L1_gnn_W_lang, L1_gnn_W_grav, L1_gnn_W_V, L1_gnn_W_O, L1_gnn_gate_logit, L1_gnn_log_sigma), axis=-1)
    return x

_drawn_inputs = setup_inputs


def setup_inputs(seed=0):
    import zlib

    import numpy as np

    out = dict(_drawn_inputs(seed))
    spreads = {'L0_gnn_bias': (0.0, 0.325)}
    factors = {'L1_gnn_W_lang': 5.222}
    for name, (base, spread) in spreads.items():
        noise = np.random.default_rng([zlib.crc32(name.encode()), seed]).standard_normal(out[name].shape)
        drawn = base * np.exp(spread * noise) if base else spread * noise
        out[name] = jnp.asarray(drawn.astype(out[name].dtype))
    for name, factor in factors.items():
        out[name] = (out[name] * factor).astype(out[name].dtype)
    return out
```

```python
from contextlib import ExitStack

import concourse.bass as bass
from concourse import mybir

F32 = mybir.dt.float32
F16 = mybir.dt.float16
ALU = mybir.AluOpType
ACT = mybir.ActivationFunctionType
X_AXIS = mybir.AxisListType.X

P = 128
EPS_LN = 1e-5
EPS_DEG = 1e-8
EPS_NORM_SQ = 1e-16
TINY = 1e-30
FP16_NORM = 2048.0


class Group:

    def __init__(self, half, parity):
        self.half, self.parity = half, parity

    def next(self):
        return Group(self.half + self.parity, 1 - self.parity)

    def prev(self):
        return Group(self.half - 1 + self.parity, 1 - self.parity)

    def count(self, per_group, n):
        return self.half * (2 * per_group) + (per_group * self.parity + n)


def resnorm_graph_kernel(nc, x, adj, bias, w_lang, w_grav, w_v, w_o, gate, log_sigma, out):
    B, N, D = x.shape
    DC = D // P
    GB = 8
    PAIRS = GB * N // P
    ROWS = GB * N
    G = B // GB
    NBLK = DC * (DC + 1) // 2
    assert N == 64 and D == 512 and G % 2 == 0 and ROWS == 512

    def blk(k, c):
        return k * (k + 1) // 2 + c

    x_dram = x.rearrange("(g u r q) n d -> g r u n q d", g=G, u=2, r=2, q=2)
    out_dram = out.rearrange("(g p q) n d -> g (q n) p d", g=G, p=PAIRS, q=2)

    ctx = ExitStack()
    with ctx:
        def sb(name, shape, dt=F32):
            return ctx.enter_context(nc.sbuf_tensor(name, shape, dt))

        def bank(name):
            return ctx.enter_context(nc.psum_tensor(name, [P, 512], F32))

        def sem(name):
            return ctx.enter_context(nc.semaphore(name))

        x_in = [sb(f"x_in{i}", [P, 2, 2, D]) for i in range(2)]
        y = sb("y", [P, PAIRS, D])
        h = [sb(f"h{i}", [P, PAIRS, D]) for i in range(2)]
        ht_hi = [sb(f"ht_hi{i}", [P, DC, ROWS], F16) for i in range(2)]
        ht_lo = [sb(f"ht_lo{i}", [P, DC, ROWS], F16) for i in range(2)]
        p_hi = sb("p_hi", [P, DC, GB, 2, N], F16)
        p_lo = sb("p_lo", [P, DC, GB, 2, N], F16)
        u = sb("u", [P, PAIRS, D])
        o = sb("o", [P, PAIRS, D])
        t_sb = sb("t_sb", [P, ROWS])
        t_diag = sb("t_diag", [P, ROWS])
        v_diag = sb("v_diag", [P, ROWS])
        s_sb = sb("s_sb", [P, ROWS])
        w_sb = sb("w_sb", [P, ROWS])
        e_sb = sb("e_sb", [P, ROWS])
        a_sb = sb("a_sb", [P, ROWS])
        ks_sb = sb("ks_sb", [P, ROWS])
        kt = sb("kt", [P, PAIRS, P])
        stats1 = sb("stats1", [P, PAIRS, 6])
        mv1 = sb("mv1", [P, PAIRS, 2])
        ve1 = sb("ve1", [P, PAIRS])
        rstd1 = sb("rstd1", [P, PAIRS])
        stats2 = sb("stats2", [P, PAIRS, 6])
        mv2 = sb("mv2", [P, PAIRS, 2])
        ve2 = sb("ve2", [P, PAIRS])
        rstd2 = sb("rstd2", [P, PAIRS])
        nmr2 = sb("nmr2", [P, PAIRS])
        diag = sb("diag", [P, GB])
        nsq = sb("nsq", [P, GB])
        vec = sb("vec", [P, GB])
        rr = sb("rr", [P, GB])
        deg = sb("deg", [P, GB])
        degr = sb("degr", [P, GB])
        degm = sb("degm", [P, GB])
        dinv = sb("dinv", [P, GB])
        cfac = sb("cfac", [P, GB])
        w_raw = {n: sb(f"w_raw_{n}", [P, DC, D]) for n in ("lang", "grav")}
        w_raw["v"] = u
        w_raw["o"] = o
        wo_t = y
        l_f32 = {"lang": sb("l_lang_f32", [P, NBLK * P]), "grav": sb("l_grav_f32", [P, NBLK * P])}
        m_f32 = h[1][:, :, :].rearrange("p a b -> p (a b)")
        square = [t[:, :, :, :, :].bitcast(F32).rearrange("p c b s n -> p (c b s n)") for t in (p_hi, p_lo)]
        l_hi = {s: sb(f"l_{s}_hi", [P, NBLK, P], F16) for s in ("lang", "grav")}
        l_lo = {s: sb(f"l_{s}_lo", [P, NBLK, P], F16) for s in ("lang", "grav")}
        m_hi = sb("m_hi", [P, DC, D], F16)
        m_lo = sb("m_lo", [P, DC, D], F16)
        ident = sb("ident", [P, P])
        ones = sb("ones", [P, P])
        ones_lg = sb("ones_lg", [P, P])
        eye2 = sb("eye2", [P, N])
        eye_g = sb("eye_g", [P, N])
        eye_l = sb("eye_l", [P, N])
        adj2 = sb("adj2", [P, N])
        adj_sq = sb("adj_sq", [P, N])
        wmix = sb("wmix", [P, N])
        not_eye = sb("not_eye", [P, N])
        mask = sb("mask", [P, N])
        bias_b = sb("bias_b", [P, D])
        gate_b = sb("gate_b", [P, 1])
        lsig_b = sb("lsig_b", [P, 1])
        gexp = sb("gexp", [P, 1])
        gexp1 = sb("gexp1", [P, 1])
        wgate = sb("wgate", [P, 1])
        wside = sb("wside", [P, 1])
        sexp = sb("sexp", [P, 1])
        cexp = sb("cexp", [P, 1])
        minus_half = sb("minus_half", [P, GB])
        eps_ln = sb("eps_ln", [P, PAIRS])
        idle_weights = sb("idle_weights", [P, P], F16)
        ssq = sb("ssq", [P, 3])
        ssq_all = sb("ssq_all", [P, 3])
        rnorm = sb("rnorm", [P, 3])
        up = sb("up", [P, 3])
        down = sb("down", [P, 3])
        t_scale = sb("t_scale", [P, 1])
        wv_scale = sb("wv_scale", [P, 1])

        front = [bank(f"front{i}") for i in range(2)]
        proj = [bank(f"proj{i}") for i in range(3)]
        ps_t = bank("ps_t")
        ps_v = bank("ps_v")
        ps_k = bank("ps_k")

        w_loaded = {n: sem(f"w_{n}_loaded") for n in ("lang", "grav", "v", "o")}
        adj_loaded = sem("adj_loaded")
        small_loaded = sem("small_loaded")
        x_loaded = [sem(f"x{i}_loaded") for i in range(2)]
        pool_const = sem("pool_const")
        dve_const = sem("dve_const")
        gw_done = sem("gw_done")
        gw_copied = sem("gw_copied")
        l_half = sem("l_half")
        wot_done = sem("wot_done")
        wot_copied = sem("wot_copied")
        act_const = sem("act_const")
        sq_summed = sem("sq_summed")
        norm_done = sem("norm_done")
        norm_copied = sem("norm_copied")
        norm_pow = sem("norm_pow")
        scale_ready = sem("scale_ready")
        wt_hi = sem("wt_hi")
        wt_lo = sem("wt_lo")
        l0_done = sem("l0_done")
        y_ready = sem("y_ready")
        stats1_ready = sem("stats1_ready")
        mv1_ready = sem("mv1_ready")
        ve1_ready = sem("ve1_ready")
        rstd1_ready = sem("rstd1_ready")
        h_ready = sem("h_ready")
        tr_done = sem("tr_done")
        hthi_ready = sem("hthi_ready")
        htlo_ready = sem("htlo_ready")
        proj_done = sem("proj_done")
        phi_ready = sem("phi_ready")
        plo_ready = sem("plo_ready")
        u_ready = sem("u_ready")
        gram_done = sem("gram_done")
        t_ready = sem("t_ready")
        tdiag_ready = sem("tdiag_ready")
        diag_ready = sem("diag_ready")
        nsq_ready = sem("nsq_ready")
        rinv_ready = sem("rinv_ready")
        rr_ready = sem("rr_ready")
        v_ready = sem("v_ready")
        sym_done = sem("sym_done")
        dj_done = sem("dj_done")
        s_ready = sem("s_ready")
        d2_ready = sem("d2_ready")
        mr_ready = sem("mr_ready")
        exp_ready = sem("exp_ready")
        a_ready = sem("a_ready")
        deg_ready = sem("deg_ready")
        ks_ready = sem("ks_ready")
        kt_done = sem("kt_done")
        kt_ready = sem("kt_ready")
        ku_done = sem("ku_done")
        sum_ready = sem("sum_ready")
        stats2_ready = sem("stats2_ready")
        mv2_ready = sem("mv2_ready")
        ve2_ready = sem("ve2_ready")
        rstd2_ready = sem("rstd2_ready")
        nmr2_ready = sem("nmr2_ready")
        out_ready = sem("out_ready")
        stored = sem("stored")

        def by_batch(tile, lo=0, hi=P):
            return tile[lo:hi, :].rearrange("p (b n) -> p b n", b=GB)

        def over_columns(small, lo=0, hi=P):
            return small[lo:hi, :].unsqueeze(2).to_broadcast([hi - lo, GB, N])

        def over_batches(square_, lo=0, hi=P):
            return square_[lo:hi, :].unsqueeze(1).to_broadcast([hi - lo, GB, N])

        L, GR = slice(0, N), slice(N, P)

        block = ctx.enter_context(nc.Block())

        @block.sync
        def _(sp):
            def load(g):
                for r in range(2):
                    for quad in range(2):
                        sp.dma_start(x_in[g.parity][r * N:(r + 1) * N, quad, :, :],
                                     x_dram[g.half * 2 + g.parity, r, quad]).then_inc(x_loaded[g.parity], 16)

            def store(g):
                sp.wait_ge(out_ready, g.count(4, 4))
                sp.dma_start(out_dram[g.half * 2 + g.parity], o[:, :, :]).then_inc(stored, 16)

            def reload(g):
                sp.wait_ge(l0_done, g.count(2, 2))
                load(Group(g.half + 1, g.parity))

            view = {n: w.rearrange("(c p) d -> p c d", p=P)
                    for n, w in (("lang", w_lang), ("grav", w_grav), ("v", w_v), ("o", w_o))}
            sp.dma_start(w_raw["lang"][:, :, :], view["lang"]).then_inc(w_loaded["lang"], 16)
            sp.dma_start(adj2[0:N, :], adj).then_inc(adj_loaded, 16)
            sp.dma_start(adj2[N:P, :], adj).then_inc(adj_loaded, 16)
            sp.dma_start(w_raw["grav"][:, :, :], view["grav"]).then_inc(w_loaded["grav"], 16)
            sp.dma_start(w_raw["o"][:, :, :], view["o"]).then_inc(w_loaded["o"], 16)
            sp.dma_start(w_raw["v"][:, :, :], view["v"]).then_inc(w_loaded["v"], 16)
            load(Group(0, 0))
            sp.dma_start(bias_b[:, :], bias.unsqueeze(0).to_broadcast([P, D])).then_inc(small_loaded, 16)
            sp.dma_start(gate_b[:, :], gate.unsqueeze(0).to_broadcast([P, 1])).then_inc(small_loaded, 16)
            sp.dma_start(lsig_b[:, :], log_sigma.unsqueeze(0).to_broadcast([P, 1])).then_inc(small_loaded, 16)
            load(Group(0, 1))
            reload(Group(0, 0))
            with sp.Fori(0, G // 2 - 2) as i:
                reload(Group(i, 1))
                store(Group(i, 0))
                reload(Group(i + 1, 0))
                store(Group(i, 1))
            last = G // 2 - 2
            reload(Group(last, 1))
            for g in (Group(last, 0), Group(last, 1), Group(last + 1, 0), Group(last + 1, 1)):
                store(g)
            sp.wait_ge(stored, 16 * G)

        def run(engine, iteration, back):
            iteration(Group(0, 0), has_prev=False, has_next=True)
            with engine.Fori(0, G // 2 - 1) as i:
                iteration(Group(i, 1), has_prev=True, has_next=True)
                iteration(Group(i + 1, 0), has_prev=True, has_next=True)
            iteration(Group(G // 2 - 1, 1), has_prev=True, has_next=False)
            back(Group(G // 2 - 1, 1))

        @block.tensor
        def _(pe):
            def mix(g, quad):
                if quad == 0:
                    pe.wait_ge(x_loaded[g.parity], g.half * 64 + 64)
                    if not (isinstance(g.half, int) and g.half == 0 and g.parity == 0):
                        pe.wait_ge(htlo_ready, g.prev().count(4, 4))
                else:
                    pe.wait_ge(y_ready, g.count(4, 2))
                pe.ldweights(idle_weights[:, :], tile_position=(0, 0))
                for r in range(2):
                    for q in range(2):
                        mm = pe.matmul(front[r][q * N:(q + 1) * N, :], wmix[r * N:(r + 1) * N, :],
                                       x_in[g.parity][r * N:(r + 1) * N, quad, q, :],
                                       start=True, stop=True)
                mm.then_inc(l0_done, 1)

            def transposes(g, p):
                pe.wait_ge(h_ready, g.count(4, p + 1))
                if p >= 2:
                    pe.wait_ge(htlo_ready, g.count(4, p - 1))
                for c in range(DC):
                    mm = pe.transpose(front[p % 2][:, c * P:(c + 1) * P],
                                      h[g.parity][:, p, c * P:(c + 1) * P], ident[:, :])
                mm.then_inc(tr_done, 1)

            def project(g, j, first):
                c, s = j % 4, ("lang", "grav")[j // 4]
                if j == 0:
                    pe.wait_ge(htlo_ready, g.count(4, 4))
                if j < 3:
                    if not first:
                        pe.wait_ge(u_ready, g.prev().count(4, j + 2))
                else:
                    pe.wait_ge(plo_ready, g.count(8, j - 2))
                passes = [(k, a, b) for k in range(c, DC)
                          for a, b in ((l_hi, ht_hi), (l_hi, ht_lo), (l_lo, ht_hi))]
                for n, (k, a, b) in enumerate(passes):
                    mm = pe.matmul(proj[j % 3][:, :], a[s][:, blk(k, c), :], b[g.parity][:, k, :],
                                   start=(n == 0), stop=(n == len(passes) - 1))
                mm.then_inc(proj_done, 1)

            def values(g, p):
                j = 8 + p
                if j < 11:
                    pe.wait_ge(plo_ready, g.count(8, j - 2))
                else:
                    pe.wait_ge(u_ready, g.count(4, 1))
                passes = [(k, a, b) for k in range(DC)
                          for a, b in ((ht_hi, m_hi), (ht_hi, m_lo), (ht_lo, m_hi))]
                for n, (k, a, b) in enumerate(passes):
                    mm = pe.matmul(proj[j % 3][:, :], a[g.parity][:, k, p * P:(p + 1) * P], b[:, k, :],
                                   start=(n == 0), stop=(n == len(passes) - 1))
                mm.then_inc(proj_done, 1)

            def gram(g, first):
                pe.wait_ge(phi_ready, g.count(8, 8))
                pe.wait_ge(plo_ready, g.count(8, 8))
                if not first:
                    pe.wait_ge(s_ready, g.prev().count(1, 1))
                passes = [(c, a, t) for c in range(DC)
                          for a, t in ((p_hi, ht_hi), (p_hi, ht_lo), (p_lo, ht_hi))]
                for b in range(GB):
                    for n, (c, a, t) in enumerate(passes):
                        mm = pe.matmul(ps_t[:, b * N:(b + 1) * N],
                                       a[:, c, b, :, :].rearrange("p s n -> p (s n)"),
                                       t[g.parity][:, c, b * N:(b + 1) * N],
                                       start=(n == 0), stop=(n == len(passes) - 1))
                mm.then_inc(gram_done, 1)

            def symmetrise(g):
                pe.wait_ge(t_ready, g.count(1, 1))
                for b in range(GB):
                    for half, eye in ((L, eye_l), (GR, eye_g)):
                        mm = pe.matmul(ps_t[half, b * N:(b + 1) * N], t_sb[:, b * N:(b + 1) * N],
                                       eye[:, :], start=True, stop=True)
                mm.then_inc(sym_done, 1)

            def spread(g, first):
                pe.wait_ge(v_ready, g.count(1, 1))
                if not first:
                    pe.wait_ge(kt_ready, g.prev().count(2, 2))
                pe.matmul(ps_v[:, :], ones_lg[:, :], v_diag[:, :], start=True, stop=True).then_inc(dj_done, 1)

            def kernel_t(g):
                pe.wait_ge(ks_ready, g.count(1, 1))
                for b in range(GB):
                    p, q = b // 2, b % 2
                    mm = pe.matmul(ps_v[q * N:(q + 1) * N, p * N:(p + 1) * N],
                                   ks_sb[:, b * N:(b + 1) * N], eye2[:, :], start=True, stop=True)
                mm.then_inc(kt_done, 1)

            def attend(g, p, first_use):
                if p == 0:
                    pe.wait_ge(kt_ready, g.count(2, 2))
                    pe.wait_ge(u_ready, g.count(4, 4))
                if not first_use:
                    pe.wait_ge(sum_ready, g.count(4, p))
                pe.matmul(ps_k[:, :], kt[:, p, :], u[:, p, :], start=True, stop=True).then_inc(ku_done, 1)

            def back(g, first=False):
                kernel_t(g)
                for p in range(PAIRS):
                    attend(g, p, first and p == 0)

            def iteration(g, has_prev, has_next):
                first = not has_prev
                before = g.prev() if has_prev else None
                first_back = has_prev and isinstance(g.half, int) and g.half == 0
                nxt = g.next() if has_next else None
                if has_next:
                    mix(nxt, 0)
                project(g, 0, first)
                if has_next:
                    mix(nxt, 1)
                project(g, 1, first)
                if has_prev:
                    kernel_t(before)
                project(g, 2, first)
                for p in range(PAIRS):
                    if has_prev:
                        attend(before, p, False)
                    project(g, 3 + p, first)
                project(g, 7, first)
                if has_next:
                    transposes(nxt, 0)
                values(g, 0)
                if has_next:
                    transposes(nxt, 1)
                gram(g, first)
                values(g, 1)
                if has_next:
                    transposes(nxt, 2)
                symmetrise(g)
                values(g, 2)
                if has_next:
                    transposes(nxt, 3)
                spread(g, first)
                values(g, 3)

            for s_n, s in enumerate(("lang", "grav")):
                pe.wait_ge(w_loaded[s], 16)
                for k in range(DC):
                    n = s_n * DC + k
                    if n >= 3:
                        pe.wait_ge(gw_copied, n - 2)
                    for e in range(DC):
                        mm = pe.matmul(proj[n % 3][:, 0:(k + 1) * P], w_raw[s][:, e, k * P:(k + 1) * P],
                                       w_raw[s][:, e, 0:(k + 1) * P], start=(e == 0), stop=(e == DC - 1))
                    mm.then_inc(gw_done, 1)
            pe.wait_ge(w_loaded["o"], 16)
            pe.wait_ge(pool_const, 2)
            for c in range(DC):
                if c >= 2:
                    pe.wait_ge(wot_copied, c - 1)
                for e in range(DC):
                    mm = pe.transpose(front[c % 2][:, e * P:(e + 1) * P],
                                      w_raw["o"][:, e, c * P:(c + 1) * P], ident[:, :])
                mm.then_inc(wot_done, 1)
            pe.wait_ge(sq_summed, 2)
            pe.wait_ge(dve_const, 1)
            pe.matmul(ps_k[:, 0:2], ones[:, :], ssq[:, 0:2], start=True, stop=True).then_inc(norm_done, 1)
            pe.wait_ge(w_loaded["v"], 16)
            pe.wait_ge(wot_copied, DC)
            for k in range(DC):
                n = 2 * DC + k
                pe.wait_ge(gw_copied, n - 2)
                for v in range(DC):
                    mm = pe.matmul(proj[n % 3][:, :], w_raw["v"][:, v, k * P:(k + 1) * P],
                                   wo_t[:, v, :], start=(v == 0), stop=(v == DC - 1))
                mm.then_inc(gw_done, 1)
            pe.wait_ge(dve_const, 3)
            pe.wait_ge(pool_const, 10)
            mix(Group(0, 0), 0)
            mix(Group(0, 0), 1)
            pe.wait_ge(sq_summed, 3)
            pe.wait_ge(norm_copied, 1)
            pe.matmul(ps_k[:, 2:3], ones[:, :], ssq[:, 2:3], start=True, stop=True).then_inc(norm_done, 1)
            for p in range(PAIRS):
                transposes(Group(0, 0), p)
            pe.wait_ge(wt_lo, 3)
            run(pe, iteration, back)

        @block.scalar
        def _(act):
            def ht_high(g, p):
                act.wait_ge(tr_done, g.count(4, p + 1))
                act.activation(ht_hi[g.parity][:, :, p * P:(p + 1) * P],
                               front[p % 2][:, :].rearrange("p (c n) -> p c n", c=DC),
                               ACT.Copy).then_inc(hthi_ready, 1)

            def p_high(g, j, first):
                if j == 0 and not first:
                    act.wait_ge(gram_done, g.prev().count(1, 1))
                act.wait_ge(proj_done, g.count(12, j + 1))
                act.activation(p_hi[:, j % 4, :, j // 4, :], by_batch(proj[j % 3]),
                               ACT.Copy).then_inc(phi_ready, 1)

            def u_copy(g, p):
                act.wait_ge(proj_done, g.count(12, 9 + p))
                act.activation(u[:, p, :], proj[(8 + p) % 3][:, :], ACT.Copy).then_inc(u_ready, 1)

            def t_copy(g, first):
                act.wait_ge(gram_done, g.count(1, 1))
                if not first:
                    act.wait_ge(s_ready, g.prev().count(1, 1))
                act.activation(t_sb[:, :], ps_t[:, :], ACT.Copy, scale=t_scale[:, 0:1]).then_inc(t_ready, 1)

            def exponent(g):
                act.wait_ge(d2_ready, g.count(2, 2))
                act.activation(e_sb[GR, :], w_sb[GR, :], ACT.Exp, scale=cexp[GR, 0:1]).then_inc(exp_ready, 1)

            def kt_copy(g):
                act.wait_ge(kt_done, g.count(1, 1))
                for q in range(2):
                    half = slice(q * N, (q + 1) * N)
                    act.activation(kt[half, :, half], ps_v[half, 0:PAIRS * N].rearrange("p (a n) -> p a n", a=PAIRS),
                                   ACT.Copy).then_inc(kt_ready, 1)

            def normalise(g, pairs):
                act.wait_ge(nmr2_ready, g.count(1, 1))
                for p in pairs:
                    act.activation(o[:, p, :], o[:, p, :], ACT.Identity, scale=rstd2[:, p:p + 1],
                                   bias=nmr2[:, p:p + 1]).then_inc(out_ready, 1)

            def back(g):
                exponent(g)
                kt_copy(g)
                normalise(g, range(PAIRS))

            def iteration(g, has_prev, has_next):
                first = not has_prev
                before = g.prev() if has_prev else None
                nxt = g.next() if has_next else None
                if has_prev:
                    exponent(before)
                p_high(g, 0, first)
                p_high(g, 1, first)
                if has_prev:
                    kt_copy(before)
                for j in range(2, 8):
                    p_high(g, j, first)
                if has_next:
                    ht_high(nxt, 0)
                u_copy(g, 0)
                if has_next:
                    ht_high(nxt, 1)
                if has_prev:
                    normalise(before, (0, 1))
                t_copy(g, first)
                u_copy(g, 1)
                if has_next:
                    ht_high(nxt, 2)
                if has_prev:
                    normalise(before, (2, 3))
                u_copy(g, 2)
                if has_next:
                    ht_high(nxt, 3)
                u_copy(g, 3)

            act.wait_ge(small_loaded, 48)
            act.activation(gexp[:, :], gate_b[:, :], ACT.Exp, scale=-1.0).then_inc(act_const, 1)
            act.activation(sexp[:, :], lsig_b[:, :], ACT.Exp, scale=-2.0).then_inc(act_const, 1)
            for s_n, s in enumerate(("lang", "grav")):
                act.wait_ge(l_half, s_n + 1)
                act.activation(square[s_n][:, 0:NBLK * P], l_f32[s][:, :], ACT.Square,
                               accum_out=ssq[:, s_n:s_n + 1]).then_inc(sq_summed, 1)
            for c in range(DC):
                act.wait_ge(wot_done, c + 1)
                act.activation(wo_t[:, c, :], front[c % 2][:, :], ACT.Copy).then_inc(wot_copied, 1)
            act.wait_ge(gw_copied, 3 * DC)
            act.wait_ge(sq_summed, 2)
            act.activation(square[0][:, 0:DC * D], m_f32, ACT.Square,
                           accum_out=ssq[:, 2:3]).then_inc(sq_summed, 1)
            for s_n, s in enumerate(("lang", "grav")):
                act.wait_ge(scale_ready, 1)
                act.activation(l_hi[s][:, :, :].rearrange("p a b -> p (a b)"), l_f32[s][:, :], ACT.Copy,
                               scale=up[:, s_n:s_n + 1]).then_inc(wt_hi, 1)
            for p in range(PAIRS):
                ht_high(Group(0, 0), p)
            act.wait_ge(scale_ready, 3)
            act.activation(m_hi[:, :, :].rearrange("p a b -> p (a b)"), m_f32, ACT.Copy,
                           scale=up[:, 2:3]).then_inc(wt_hi, 1)
            act.wait_ge(sq_summed, 3)
            act.wait_ge(scale_ready, 4)
            run(act, iteration, back)

        @block.vector
        def _(dve):
            def add_bias(g, quad):
                dve.wait_ge(l0_done, g.count(2, quad + 1))
                for r in range(2):
                    dve.tensor_tensor(y[:, 2 * quad + r, :], front[r][:, :], bias_b[:, :],
                                      ALU.add).then_inc(y_ready, 1)

            def row_stats(g, quad):
                for r in range(2):
                    p = 2 * quad + r
                    dve.wait_ge(y_ready, g.count(4, p + 1))
                    dve.bn_stats(stats1[:, p, :], y[:, p, :]).then_inc(stats1_ready, 1)

            def row_moments(g):
                for p in range(PAIRS):
                    dve.bn_aggr(mv1[:, p, :], stats1[:, p, :]).then_inc(mv1_ready, 1)

            def norm_rows(g):
                dve.wait_ge(rstd1_ready, g.count(1, 1))
                for p in range(PAIRS):
                    dve.tensor_scalar(h[g.parity][:, p, :], y[:, p, :], mv1[:, p, 0:1], rstd1[:, p:p + 1],
                                      ALU.subtract, ALU.mult).then_inc(h_ready, 1)

            def ht_low(g, p):
                cols = slice(p * P, (p + 1) * P)
                dve.wait_ge(hthi_ready, g.count(4, p + 1))
                dve.tensor_tensor(ht_lo[g.parity][:, :, cols],
                                  front[p % 2][:, :].rearrange("p (c n) -> p c n", c=DC),
                                  ht_hi[g.parity][:, :, cols], ALU.subtract).then_inc(htlo_ready, 1)

            def p_low(g, j):
                dve.wait_ge(phi_ready, g.count(8, j + 1))
                dve.tensor_tensor(p_lo[:, j % 4, :, j // 4, :], by_batch(proj[j % 3]),
                                  p_hi[:, j % 4, :, j // 4, :], ALU.subtract).then_inc(plo_ready, 1)

            def diagonals(g):
                dve.wait_ge(tdiag_ready, g.count(1, 1))
                dve.reduce_sum(diag[:, :], by_batch(t_diag), X_AXIS).then_inc(diag_ready, 1)
                dve.wait_ge(diag_ready, g.count(1, 1))
                dve.tensor_scalar(nsq[L, :], diag[L, :], 2.0, EPS_NORM_SQ, ALU.mult, ALU.max).then_inc(nsq_ready, 1)
                dve.tensor_scalar(vec[GR, :], diag[GR, :], 2.0, None, ALU.mult).then_inc(nsq_ready, 1)

            def diagonal_matrices(g):
                dve.wait_ge(rinv_ready, g.count(1, 1))
                dve.wait_ge(nsq_ready, g.count(2, 2))
                dve.tensor_tensor(by_batch(v_diag), over_batches(eye2), over_columns(vec),
                                  ALU.mult).then_inc(v_ready, 1)

            def distances(g):
                dve.wait_ge(sym_done, g.count(1, 1))
                dve.tensor_tensor(s_sb[:, :], ps_t[:, :], t_sb[:, :], ALU.add).then_inc(s_ready, 1)
                dve.wait_ge(dj_done, g.count(1, 1))
                dve.wait_ge(s_ready, g.count(1, 1))
                dve.scalar_tensor_tensor(out=s_sb[GR, :], in0=s_sb[GR, :], scalar=-2.0, in1=ps_v[GR, :],
                                         op0=ALU.mult, op1=ALU.add).then_inc(d2_ready, 1)
                dve.tensor_tensor(by_batch(w_sb, 0, N), by_batch(ps_v, 0, N), over_batches(mask, 0, N),
                                  ALU.mult).then_inc(mr_ready, 1)
                dve.wait_ge(d2_ready, g.count(2, 1))
                dve.tensor_tensor(by_batch(w_sb, N, P), by_batch(s_sb, N, P), over_columns(vec, N, P),
                                  ALU.add).then_inc(d2_ready, 1)

            def similarities(g):
                dve.wait_ge(mr_ready, g.count(1, 1))
                dve.scalar_tensor_tensor(out=a_sb[L, :], in0=s_sb[L, :], scalar=0.0, in1=w_sb[L, :],
                                         op0=ALU.max, op1=ALU.mult).then_inc(a_ready, 1)

            def gravities(g):
                dve.wait_ge(exp_ready, g.count(1, 1))
                dve.scalar_tensor_tensor(out=by_batch(a_sb, N, P), in0=by_batch(e_sb, N, P), scalar=1.0,
                                         in1=over_batches(mask, N, P), op0=ALU.min,
                                         op1=ALU.mult).then_inc(a_ready, 1)

            def row_factors(g):
                dve.wait_ge(a_ready, g.count(2, 2))
                dve.reduce_sum(deg[:, :], by_batch(a_sb), X_AXIS).then_inc(deg_ready, 1)
                dve.wait_ge(deg_ready, g.count(5, 1))
                dve.wait_ge(rr_ready, g.count(1, 1))
                dve.tensor_tensor(degr[:, :], deg[:, :], rr[:, :], ALU.mult).then_inc(deg_ready, 1)
                dve.wait_ge(deg_ready, g.count(5, 2))
                dve.tensor_scalar(degm[:, :], degr[:, :], EPS_DEG, None, ALU.max).then_inc(deg_ready, 1)
                dve.wait_ge(deg_ready, g.count(5, 3))
                dve.reciprocal(dinv[:, :], degm[:, :]).then_inc(deg_ready, 1)
                dve.wait_ge(deg_ready, g.count(5, 4))
                dve.scalar_tensor_tensor(out=cfac[:, :], in0=dinv[:, :], scalar=wv_scale[:, 0:1], in1=rr[:, :],
                                         op0=ALU.mult, op1=ALU.mult).then_inc(deg_ready, 1)

            def scale_rows(g):
                dve.wait_ge(deg_ready, g.count(5, 5))
                dve.tensor_tensor(by_batch(ks_sb), by_batch(a_sb), over_columns(cfac), ALU.mult).then_inc(ks_ready, 1)

            def residual(g, p, first):
                dve.wait_ge(ku_done, g.count(4, p + 1))
                if p == 0 and not first:
                    dve.wait_ge(stored, g.prev().count(16, 16))
                dve.tensor_tensor(o[:, p, :], ps_k[:, :], h[g.parity][:, p, :], ALU.add).then_inc(sum_ready, 1)

            def out_stats(g, p):
                dve.wait_ge(sum_ready, g.count(4, p + 1))
                dve.bn_stats(stats2[:, p, :], o[:, p, :]).then_inc(stats2_ready, 1)

            def out_moments(g):
                for p in range(PAIRS):
                    dve.bn_aggr(mv2[:, p, :], stats2[:, p, :]).then_inc(mv2_ready, 1)

            def out_shift(g):
                dve.wait_ge(rstd2_ready, g.count(1, 1))
                dve.scalar_tensor_tensor(out=nmr2[:, :], in0=mv2[:, :, 0], scalar=-1.0, in1=rstd2[:, :],
                                         op0=ALU.mult, op1=ALU.mult).then_inc(nmr2_ready, 1)

            def back(g):
                distances(g)
                similarities(g)
                gravities(g)
                row_factors(g)
                scale_rows(g)
                for p in range(PAIRS):
                    residual(g, p, False)
                    out_stats(g, p)
                dve.wait_ge(stats2_ready, g.count(4, 4))
                out_moments(g)
                out_shift(g)

            def iteration(g, has_prev, has_next):
                before = g.prev() if has_prev else None
                nxt = g.next() if has_next else None
                first_store = isinstance(g.half, int) and g.half == 0
                if has_prev:
                    distances(before)
                if has_next:
                    add_bias(nxt, 0)
                if has_prev:
                    similarities(before)
                if has_next:
                    row_stats(nxt, 0)
                p_low(g, 0)
                if has_prev:
                    gravities(before)
                    row_factors(before)
                    scale_rows(before)
                if has_next:
                    add_bias(nxt, 1)
                    row_stats(nxt, 1)
                    dve.wait_ge(stats1_ready, nxt.count(4, 4))
                p_low(g, 1)
                if has_next:
                    row_moments(nxt)
                p_low(g, 2)
                for p in range(PAIRS):
                    if has_prev:
                        residual(before, p, has_prev == "first")
                    p_low(g, 3 + p)
                    if has_prev:
                        out_stats(before, p)
                if has_next:
                    norm_rows(nxt)
                if has_prev:
                    dve.wait_ge(stats2_ready, before.count(4, 4))
                p_low(g, 7)
                if has_prev:
                    out_moments(before)
                if has_next:
                    ht_low(nxt, 0)
                    ht_low(nxt, 1)
                if has_prev:
                    out_shift(before)
                diagonals(g)
                if has_next:
                    ht_low(nxt, 2)
                diagonal_matrices(g)
                if has_next:
                    ht_low(nxt, 3)

            dve.memset(ones[:, :], 1.0).then_inc(dve_const, 1)
            dve.wait_ge(adj_loaded, 32)
            dve.tensor_tensor(adj_sq[:, :], adj2[:, :], adj2[:, :], ALU.mult).then_inc(dve_const, 1)
            dve.wait_ge(dve_const, 2)
            dve.wait_ge(pool_const, 4)
            dve.tensor_tensor(wmix[:, :], adj_sq[:, :], eye2[:, :], ALU.add).then_inc(dve_const, 1)
            dve.tensor_scalar(not_eye[:, :], eye2[:, :], -1.0, 1.0, ALU.mult, ALU.add).then_inc(dve_const, 1)
            dve.wait_ge(dve_const, 4)
            dve.tensor_tensor(mask[:, :], adj2[:, :], not_eye[:, :], ALU.mult).then_inc(dve_const, 1)
            dve.tensor_copy(eye_l[:, :], ident[:, 0:N]).then_inc(dve_const, 1)
            dve.tensor_copy(eye_g[:, :], ident[:, N:P]).then_inc(dve_const, 1)
            dve.memset(minus_half[:, :], -0.5).then_inc(dve_const, 1)
            dve.memset(rr[:, :], 1.0).then_inc(dve_const, 1)
            for s_n, s in enumerate(("lang", "grav")):
                for k in range(DC):
                    n = s_n * DC + k
                    dve.wait_ge(gw_done, n + 1)
                    if k:
                        dve.tensor_copy(l_f32[s][:, blk(k, 0) * P:blk(k, k) * P], proj[n % 3][:, 0:k * P])
                    done = dve.tensor_scalar(l_f32[s][:, blk(k, k) * P:(blk(k, k) + 1) * P],
                                             proj[n % 3][:, k * P:(k + 1) * P], 0.5, None, ALU.mult)
                    done.then_inc(gw_copied, 1)
                dve.wait_ge(gw_copied, DC * (s_n + 1))
                dve.memset(gexp1[:, :], 0.0).then_inc(l_half, 1)
            dve.wait_ge(act_const, 2)
            dve.wait_ge(l_half, 2)
            dve.tensor_scalar(gexp1[:, :], gexp[:, :], 1.0, None, ALU.add).then_inc(dve_const, 1)
            dve.tensor_scalar(cexp[:, :], sexp[:, :], -0.5, None, ALU.mult).then_inc(dve_const, 1)
            dve.wait_ge(dve_const, 11)
            dve.reciprocal(wgate[:, :], gexp1[:, :]).then_inc(dve_const, 1)
            dve.wait_ge(dve_const, 12)
            dve.tensor_copy(wside[L, :], wgate[L, :]).then_inc(dve_const, 1)
            dve.tensor_scalar(wside[GR, :], wgate[GR, :], -1.0, 1.0, ALU.mult, ALU.add).then_inc(dve_const, 1)
            dve.wait_ge(norm_done, 1)
            dve.tensor_scalar(ssq_all[:, 0:2], ps_k[:, 0:2], TINY, None, ALU.max).then_inc(norm_copied, 1)
            dve.wait_ge(norm_pow, 1)
            dve.tensor_scalar(up[:, 0:2], rnorm[:, 0:2], FP16_NORM, None, ALU.mult).then_inc(scale_ready, 1)
            dve.wait_ge(scale_ready, 1)
            dve.reciprocal(down[:, 0:2], up[:, 0:2]).then_inc(scale_ready, 1)
            for k in range(DC):
                n = 2 * DC + k
                dve.wait_ge(gw_done, n + 1)
                dve.tensor_copy(m_f32[:, k * D:(k + 1) * D], proj[n % 3][:, :]).then_inc(gw_copied, 1)
            for s_n, s in enumerate(("lang", "grav")):
                dve.wait_ge(wt_hi, s_n + 1)
                dve.scalar_tensor_tensor(out=l_lo[s][:, :, :].rearrange("p a b -> p (a b)"), in0=l_f32[s][:, :],
                                         scalar=up[:, s_n:s_n + 1],
                                         in1=l_hi[s][:, :, :].rearrange("p a b -> p (a b)"),
                                         op0=ALU.mult, op1=ALU.subtract).then_inc(wt_lo, 1)
            dve.wait_ge(small_loaded, 48)
            g0 = Group(0, 0)
            for quad in range(2):
                add_bias(g0, quad)
                row_stats(g0, quad)
            dve.wait_ge(stats1_ready, 4)
            row_moments(g0)
            dve.wait_ge(norm_done, 2)
            dve.tensor_scalar(ssq_all[:, 2:3], ps_k[:, 2:3], TINY, None, ALU.max).then_inc(norm_copied, 1)
            norm_rows(g0)
            dve.wait_ge(norm_pow, 2)
            dve.tensor_scalar(up[:, 2:3], rnorm[:, 2:3], FP16_NORM, None, ALU.mult).then_inc(scale_ready, 1)
            dve.wait_ge(scale_ready, 3)
            dve.reciprocal(down[:, 2:3], up[:, 2:3]).then_inc(scale_ready, 1)
            dve.wait_ge(scale_ready, 4)
            dve.tensor_copy(t_scale[L, :], down[L, 0:1])
            dve.tensor_copy(t_scale[GR, :], down[GR, 1:2])
            dve.wait_ge(dve_const, 14)
            dve.tensor_tensor(wv_scale[:, :], wside[:, :], down[:, 2:3], ALU.mult).then_inc(scale_ready, 1)
            for p in range(PAIRS):
                ht_low(g0, p)
            dve.wait_ge(wt_hi, 3)
            dve.scalar_tensor_tensor(out=m_lo[:, :, :].rearrange("p a b -> p (a b)"), in0=m_f32,
                                     scalar=up[:, 2:3], in1=m_hi[:, :, :].rearrange("p a b -> p (a b)"),
                                     op0=ALU.mult, op1=ALU.subtract).then_inc(wt_lo, 1)
            run(dve, iteration, back)

        @block.gpsimd
        def _(pool):
            def inverse_std(g, mv_ready, mv, ve_ready, ve, rstd_ready, rstd):
                pool.wait_ge(mv_ready, g.count(4, 4))
                pool.tensor_tensor(ve[:, :], mv[:, :, 1], eps_ln[:, :], ALU.add).then_inc(ve_ready, 1)
                pool.wait_ge(ve_ready, g.count(1, 1))
                pool.tensor_tensor(rstd[:, :], ve[:, :], minus_half[:, 0:PAIRS], ALU.pow).then_inc(rstd_ready, 1)

            def ln1(g):
                inverse_std(g, mv1_ready, mv1, ve1_ready, ve1, rstd1_ready, rstd1)

            def ln2(g):
                inverse_std(g, mv2_ready, mv2, ve2_ready, ve2, rstd2_ready, rstd2)

            def t_diagonal(g):
                pool.wait_ge(t_ready, g.count(1, 1))
                pool.tensor_tensor(by_batch(t_diag), by_batch(t_sb), over_batches(eye2),
                                   ALU.mult).then_inc(tdiag_ready, 1)

            def inverse_norm(g):
                pool.wait_ge(nsq_ready, g.count(2, 1))
                pool.tensor_tensor(vec[L, :], nsq[L, :], minus_half[L, :], ALU.pow).then_inc(rinv_ready, 1)
                pool.tensor_tensor(rr[L, :], nsq[L, :], minus_half[L, :], ALU.pow).then_inc(rr_ready, 1)

            def iteration(g, has_prev, has_next):
                if has_next:
                    ln1(g.next())
                if has_prev:
                    ln2(g.prev())
                t_diagonal(g)
                inverse_norm(g)

            pool.memset(ident[:, :], 0.0).then_inc(pool_const, 1)
            pool.wait_ge(pool_const, 1)
            pool.affine_select(out=ident[:, :], in_=ident[:, :], compare_op=ALU.not_equal, fill=1.0, base=0,
                               pattern=[[-1, P]], channel_multiplier=1).then_inc(pool_const, 1)
            pool.wait_ge(pool_const, 2)
            pool.tensor_copy(eye2[L, :], ident[L, 0:N]).then_inc(pool_const, 1)
            pool.wait_ge(pool_const, 3)
            pool.tensor_copy(eye2[GR, :], ident[GR, N:P]).then_inc(pool_const, 1)
            pool.wait_ge(pool_const, 4)
            pool.memset(ones_lg[:, :], 0.0).then_inc(pool_const, 1)
            pool.wait_ge(pool_const, 5)
            pool.memset(ones_lg[L, 0:N], 1.0).then_inc(pool_const, 1)
            pool.wait_ge(pool_const, 6)
            pool.memset(ones_lg[GR, N:P], 1.0).then_inc(pool_const, 1)
            pool.wait_ge(pool_const, 7)
            pool.memset(kt[:, :, :], 0.0).then_inc(pool_const, 1)
            pool.memset(eps_ln[:, :], EPS_LN).then_inc(pool_const, 1)
            pool.memset(idle_weights[:, :], 0.0).then_inc(pool_const, 1)
            pool.wait_ge(pool_const, 10)
            pool.wait_ge(dve_const, 8)
            pool.wait_ge(norm_copied, 1)
            pool.tensor_tensor(rnorm[:, 0:2], ssq_all[:, 0:2], minus_half[:, 0:2], ALU.pow).then_inc(norm_pow, 1)
            ln1(Group(0, 0))
            pool.wait_ge(norm_copied, 2)
            pool.tensor_tensor(rnorm[:, 2:3], ssq_all[:, 2:3], minus_half[:, 2:3], ALU.pow).then_inc(norm_pow, 1)
            run(pool, iteration, ln2)


_INS = ["x", "adj", "L0_gnn_bias", "L1_gnn_W_lang", "L1_gnn_W_grav", "L1_gnn_W_V", "L1_gnn_W_O",
        "L1_gnn_gate_logit", "L1_gnn_log_sigma"]


def kernel(**inputs):
    import numpy as np
    import concourse.bacc as bacc
    from concourse.bass_utils import run_bass_kernel_spmd

    nc = bacc.Bacc("TRN2", target_bir_lowering=False, num_devices=1)
    arrays, args = {}, []
    for name in _INS:
        a = np.ascontiguousarray(inputs[name])
        arrays[f"in_{name}"] = a
        args.append(nc.dram_tensor(f"in_{name}", a.shape, mybir.dt.from_np(a.dtype), kind="ExternalInput").ap())
    shape = inputs["x"].shape
    out = nc.dram_tensor("out", shape, F32, kind="ExternalOutput").ap()
    resnorm_graph_kernel(nc, *args, out)
    r = run_bass_kernel_spmd(nc, [arrays], core_ids=[0])
    return r.results[0]["out"]
```

```python
from contextlib import ExitStack

import concourse.bass as bass
from concourse import mybir

F32 = mybir.dt.float32
F16 = mybir.dt.float16
ALU = mybir.AluOpType
ACT = mybir.ActivationFunctionType
X_AXIS = mybir.AxisListType.X

P = 128
EPS_LN = 1e-5
EPS_DEG = 1e-8
EPS_NORM_SQ = 1e-16
TINY = 1e-30
FP16_NORM = 2048.0


class Group:

    def __init__(self, half, parity):
        self.half, self.parity = half, parity

    def next(self):
        return Group(self.half + self.parity, 1 - self.parity)

    def prev(self):
        return Group(self.half - 1 + self.parity, 1 - self.parity)

    def count(self, per_group, n):
        return self.half * (2 * per_group) + (per_group * self.parity + n)


def resnorm_graph_kernel(nc, x, adj, bias, w_lang, w_grav, w_v, w_o, gate, log_sigma, out):
    B, N, D = x.shape
    DC = D // P
    GB = 8
    PAIRS = GB * N // P
    ROWS = GB * N
    G = B // GB
    NBLK = DC * (DC + 1) // 2
    g_last_out = PAIRS * (G - 1)
    assert N == 64 and D == 512 and G % 2 == 0 and ROWS == 512

    def blk(k, c):
        return k * (k + 1) // 2 + c

    x_dram = x.rearrange("(g p q) n d -> g (q n) p d", g=G, p=PAIRS, q=2)
    out_dram = out.rearrange("(g p q) n d -> g (q n) p d", g=G, p=PAIRS, q=2)

    ctx = ExitStack()
    with ctx:
        def sb(name, shape, dt=F32):
            return ctx.enter_context(nc.sbuf_tensor(name, shape, dt))

        def bank(name):
            return ctx.enter_context(nc.psum_tensor(name, [P, 512], F32))

        def sem(name):
            return ctx.enter_context(nc.semaphore(name))

        x_in = [sb(f"x_in{i}", [P, PAIRS, D]) for i in range(2)]
        y = sb("y", [P, PAIRS, D])
        h = [sb(f"h{i}", [P, PAIRS, D]) for i in range(2)]
        h_hi = sb("h_hi", [P, PAIRS, D], F16)
        h_lo = sb("h_lo", [P, PAIRS, D], F16)
        ht_hi = [sb(f"ht_hi{i}", [P, DC, ROWS], F16) for i in range(2)]
        ht_lo = [sb(f"ht_lo{i}", [P, DC, ROWS], F16) for i in range(2)]
        p_hi = sb("p_hi", [P, DC, GB, 2, N], F16)
        p_lo = sb("p_lo", [P, DC, GB, 2, N], F16)
        u = sb("u", [P, PAIRS, D])
        o = sb("o", [P, PAIRS, D])
        t_sb = sb("t_sb", [P, ROWS])
        t_diag = sb("t_diag", [P, ROWS])
        v_diag = sb("v_diag", [P, ROWS])
        s_sb = sb("s_sb", [P, ROWS])
        w_sb = sb("w_sb", [P, ROWS])
        e_sb = sb("e_sb", [P, ROWS])
        a_sb = sb("a_sb", [P, ROWS])
        ks_sb = sb("ks_sb", [P, ROWS])
        kt = sb("kt", [P, PAIRS, P])
        stats1 = sb("stats1", [P, PAIRS, 6])
        mv1 = sb("mv1", [P, PAIRS, 2])
        ve1 = sb("ve1", [P, PAIRS])
        rstd1 = sb("rstd1", [P, PAIRS])
        stats2 = sb("stats2", [P, PAIRS, 6])
        mv2 = sb("mv2", [P, PAIRS, 2])
        ve2 = sb("ve2", [P, PAIRS])
        rstd2 = sb("rstd2", [P, PAIRS])
        nmr2 = sb("nmr2", [P, PAIRS])
        diag = sb("diag", [P, GB])
        nsq = sb("nsq", [P, GB])
        vec = sb("vec", [P, GB])
        rr = sb("rr", [P, GB])
        deg = sb("deg", [P, GB])
        degr = sb("degr", [P, GB])
        degm = sb("degm", [P, GB])
        dinv = sb("dinv", [P, GB])
        cfac = sb("cfac", [P, GB])
        w_raw = {n: sb(f"w_raw_{n}", [P, DC, D]) for n in ("lang", "grav")}
        w_raw["v"] = u
        w_raw["o"] = o
        wo_t = sb("wo_t", [P, DC, D])
        l_f32 = {"lang": sb("l_lang_f32", [P, NBLK * P]), "grav": sb("l_grav_f32", [P, NBLK * P])}
        m_f32 = sb("m_f32", [P, DC * D])[:, :]
        square = [t[:, :, :, :, :].bitcast(F32).rearrange("p c b s n -> p (c b s n)") for t in (p_hi, p_lo)]
        l_hi = {s: sb(f"l_{s}_hi", [P, NBLK, P], F16) for s in ("lang", "grav")}
        l_lo = {s: sb(f"l_{s}_lo", [P, NBLK, P], F16) for s in ("lang", "grav")}
        m_hi = sb("m_hi", [P, DC, D], F16)
        m_lo = sb("m_lo", [P, DC, D], F16)
        ident = sb("ident", [P, P])
        ones = sb("ones", [P, P])
        ones_lg = sb("ones_lg", [P, P])
        eye2 = sb("eye2", [P, N])
        eye_g = sb("eye_g", [P, N])
        eye_l = sb("eye_l", [P, N])
        adj2 = sb("adj2", [P, N])
        adj_sq = sb("adj_sq", [P, N])
        wmix = sb("wmix", [P, P])
        not_eye = sb("not_eye", [P, N])
        mask = sb("mask", [P, N])
        bias_b = sb("bias_b", [P, D])
        gate_b = sb("gate_b", [P, 1])
        lsig_b = sb("lsig_b", [P, 1])
        gexp = sb("gexp", [P, 1])
        gexp1 = sb("gexp1", [P, 1])
        wgate = sb("wgate", [P, 1])
        wside = sb("wside", [P, 1])
        sexp = sb("sexp", [P, 1])
        cexp = sb("cexp", [P, 1])
        minus_half = sb("minus_half", [P, GB])
        eps_ln = sb("eps_ln", [P, PAIRS])
        ssq = sb("ssq", [P, 3])
        ssq_all = sb("ssq_all", [P, 3])
        rnorm = sb("rnorm", [P, 3])
        up = sb("up", [P, 3])
        down = sb("down", [P, 3])
        t_scale = sb("t_scale", [P, 1])
        wv_scale = sb("wv_scale", [P, 1])

        front = [bank(f"front{i}") for i in range(2)]
        proj = [bank(f"proj{i}") for i in range(3)]
        ps_t = bank("ps_t")
        ps_v = bank("ps_v")
        ps_k = bank("ps_k")
        ku_bank = [ps_k, *front, ps_k]

        w_loaded = {n: sem(f"w_{n}_loaded") for n in ("lang", "grav", "v", "o")}
        adj_loaded = sem("adj_loaded")
        bias_loaded = sem("bias_loaded")
        small_loaded = sem("small_loaded")
        x_loaded = [sem(f"x{i}_loaded") for i in range(2)]
        pool_const = sem("pool_const")
        dve_const = sem("dve_const")
        half_ready = sem("half_ready")
        gw_done = sem("gw_done")
        gw_copied = sem("gw_copied")
        wot_done = sem("wot_done")
        wot_copied = sem("wot_copied")
        act_const = sem("act_const")
        sq_summed = sem("sq_summed")
        norm_done = sem("norm_done")
        norm_copied = sem("norm_copied")
        norm_pow = sem("norm_pow")
        scale_ready = sem("scale_ready")
        t_scale_ready = sem("t_scale_ready")
        wt_hi = sem("wt_hi")
        wt_lo = sem("wt_lo")
        l0_done = sem("l0_done")
        y_ready = sem("y_ready")
        stats1_ready = sem("stats1_ready")
        mv1_ready = sem("mv1_ready")
        ve1_ready = sem("ve1_ready")
        rstd1_ready = sem("rstd1_ready")
        h_ready = sem("h_ready")
        hhi_ready = sem("hhi_ready")
        hlo_ready = sem("hlo_ready")
        ht_loaded = [sem(f"ht{i}_loaded") for i in range(2)]
        proj_done = sem("proj_done")
        phi_ready = sem("phi_ready")
        plo_ready = sem("plo_ready")
        u_ready = sem("u_ready")
        gram_done = sem("gram_done")
        t_ready = sem("t_ready")
        tdiag_ready = sem("tdiag_ready")
        diag_ready = sem("diag_ready")
        nsq_ready = sem("nsq_ready")
        rinv_ready = sem("rinv_ready")
        rr_ready = sem("rr_ready")
        v_ready = sem("v_ready")
        sym_done = sem("sym_done")
        dj_done = sem("dj_done")
        s_ready = sem("s_ready")
        d2_ready = sem("d2_ready")
        mr_ready = sem("mr_ready")
        exp_ready = sem("exp_ready")
        a_ready = sem("a_ready")
        deg_ready = sem("deg_ready")
        ks_ready = sem("ks_ready")
        kt_done = sem("kt_done")
        kt_ready = sem("kt_ready")
        ku_done = sem("ku_done")
        sum_ready = sem("sum_ready")
        stats2_ready = sem("stats2_ready")
        mv2_ready = sem("mv2_ready")
        ve2_ready = sem("ve2_ready")
        rstd2_ready = sem("rstd2_ready")
        nmr2_ready = sem("nmr2_ready")
        out_ready = sem("out_ready")
        out_ready_dve = sem("out_ready_dve")
        stored = sem("stored")

        def by_batch(tile, lo=0, hi=P):
            return tile[lo:hi, :].rearrange("p (b n) -> p b n", b=GB)

        def over_columns(small, lo=0, hi=P):
            return small[lo:hi, :].unsqueeze(2).to_broadcast([hi - lo, GB, N])

        def over_batches(square_, lo=0, hi=P):
            return square_[lo:hi, :].unsqueeze(1).to_broadcast([hi - lo, GB, N])

        L, GR = slice(0, N), slice(N, P)

        block = ctx.enter_context(nc.Block())

        @block.sync
        def _(sp):
            def load(g):
                sp.dma_start(x_in[g.parity][:, :, :], x_dram[g.half * 2 + g.parity]).then_inc(x_loaded[g.parity], 16)

            def store(g):
                sp.wait_ge(out_ready, g.count(4, 4))
                sp.dma_start(out_dram[g.half * 2 + g.parity], o[:, :, :]).then_inc(stored, 16)

            def reload(g):
                sp.wait_ge(l0_done, g.count(4, 4))
                load(Group(g.half + 1, g.parity))

            view = {n: w.rearrange("(c p) d -> p c d", p=P)
                    for n, w in (("lang", w_lang), ("grav", w_grav), ("v", w_v), ("o", w_o))}
            sp.dma_start(adj2[0:N, :], adj).then_inc(adj_loaded, 16)
            sp.dma_start(adj2[N:P, :], adj).then_inc(adj_loaded, 16)
            load(Group(0, 0))
            sp.dma_start(bias_b[:, :], bias.unsqueeze(0).to_broadcast([P, D])).then_inc(bias_loaded, 16)
            for n in ("lang", "grav", "o", "v"):
                sp.dma_start(w_raw[n][:, :, :], view[n]).then_inc(w_loaded[n], 16)
            sp.dma_start(gate_b[:, :], gate.unsqueeze(0).to_broadcast([P, 1])).then_inc(small_loaded, 16)
            sp.dma_start(lsig_b[:, :], log_sigma.unsqueeze(0).to_broadcast([P, 1])).then_inc(small_loaded, 16)
            load(Group(0, 1))
            reload(Group(0, 0))
            with sp.Fori(0, G // 2 - 2) as i:
                reload(Group(i, 1))
                store(Group(i, 0))
                reload(Group(i + 1, 0))
                store(Group(i, 1))
            last = G // 2 - 2
            reload(Group(last, 1))
            for g in (Group(last, 0), Group(last, 1), Group(last + 1, 0)):
                store(g)
            end = Group(last + 1, 1)
            for n, p in enumerate((0, 2, 1, 3)):
                sp.wait_ge((out_ready, out_ready_dve)[p // 2], (g_last_out, 0)[p // 2] + p % 2 + 1)
                sp.dma_start(out_dram[2 * end.half + end.parity][:, p, :], o[:, p, :]).then_inc(stored, 16)
            sp.wait_ge(stored, 16 * (G - 1 + PAIRS))

        def run(engine, iteration, back):
            iteration(Group(0, 0), has_prev=False, has_next=True)
            with engine.Fori(0, G // 2 - 1) as i:
                iteration(Group(i, 1), has_prev=True, has_next=True)
                iteration(Group(i + 1, 0), has_prev=True, has_next=True)
            iteration(Group(G // 2 - 1, 1), has_prev=True, has_next=False)
            back(Group(G // 2 - 1, 1))

        @block.tensor
        def _(pe):
            def mix(g, p, first=False):
                if p == 0:
                    pe.wait_ge(x_loaded[g.parity], g.half * 16 + 16)
                if p >= 2:
                    pe.wait_ge(y_ready, g.count(4, p - 1))
                elif not first:
                    pe.wait_ge(h_ready, g.prev().count(4, 1))
                pe.matmul(front[p % 2][:, :], wmix[:, :], x_in[g.parity][:, p, :],
                          start=True, stop=True).then_inc(l0_done, 1)

            def project(g, j, first):
                c, s = j % 4, ("lang", "grav")[j // 4]
                if j == 0:
                    pe.wait_ge(ht_loaded[g.parity], g.half * 128 + 128)
                if j < 3:
                    if not first:
                        pe.wait_ge(u_ready, g.prev().count(4, j + 2))
                else:
                    pe.wait_ge(plo_ready, g.count(8, j - 2))
                passes = [(k, a, b) for k in range(c, DC)
                          for a, b in ((l_hi, ht_hi), (l_hi, ht_lo), (l_lo, ht_hi))]
                for n, (k, a, b) in enumerate(passes):
                    mm = pe.matmul(proj[j % 3][:, :], a[s][:, blk(k, c), :], b[g.parity][:, k, :],
                                   start=(n == 0), stop=(n == len(passes) - 1))
                mm.then_inc(proj_done, 1)

            def values(g, p):
                j = 8 + p
                if j < 11:
                    pe.wait_ge(plo_ready, g.count(8, j - 2))
                else:
                    pe.wait_ge(u_ready, g.count(4, 1))
                passes = [(k, a, b) for k in range(DC)
                          for a, b in ((ht_hi, m_hi), (ht_hi, m_lo), (ht_lo, m_hi))]
                for n, (k, a, b) in enumerate(passes):
                    mm = pe.matmul(proj[j % 3][:, :], a[g.parity][:, k, p * P:(p + 1) * P], b[:, k, :],
                                   start=(n == 0), stop=(n == len(passes) - 1))
                mm.then_inc(proj_done, 1)

            def gram(g, first):
                pe.wait_ge(phi_ready, g.count(8, 8))
                pe.wait_ge(plo_ready, g.count(8, 8))
                if not first:
                    pe.wait_ge(s_ready, g.prev().count(1, 1))
                passes = [(c, a, t) for c in range(DC)
                          for a, t in ((p_hi, ht_hi), (p_hi, ht_lo), (p_lo, ht_hi))]
                for b in range(GB):
                    for n, (c, a, t) in enumerate(passes):
                        mm = pe.matmul(ps_t[:, b * N:(b + 1) * N],
                                       a[:, c, b, :, :].rearrange("p s n -> p (s n)"),
                                       t[g.parity][:, c, b * N:(b + 1) * N],
                                       start=(n == 0), stop=(n == len(passes) - 1))
                mm.then_inc(gram_done, 1)

            def symmetrise(g):
                pe.wait_ge(t_ready, g.count(1, 1))
                for b in range(GB):
                    for half, eye in ((L, eye_l), (GR, eye_g)):
                        mm = pe.matmul(ps_t[half, b * N:(b + 1) * N], t_sb[:, b * N:(b + 1) * N],
                                       eye[:, :], start=True, stop=True)
                mm.then_inc(sym_done, 1)

            def spread(g, first):
                pe.wait_ge(v_ready, g.count(1, 1))
                if not first:
                    pe.wait_ge(kt_ready, g.prev().count(2, 2))
                pe.matmul(ps_v[:, :], ones_lg[:, :], v_diag[:, :], start=True, stop=True).then_inc(dj_done, 1)

            def kernel_t(g):
                pe.wait_ge(ks_ready, g.count(1, 1))
                for b in range(GB):
                    p, q = b // 2, b % 2
                    mm = pe.matmul(ps_v[q * N:(q + 1) * N, p * N:(p + 1) * N],
                                   ks_sb[:, b * N:(b + 1) * N], eye2[:, :], start=True, stop=True)
                mm.then_inc(kt_done, 1)

            def attend(g, p, to=None, mixed=None):
                if mixed and p in (1, 2):
                    pe.wait_ge(y_ready, mixed.count(4, p + 2))
                if p == 0:
                    pe.wait_ge(kt_ready, g.count(2, 2))
                    pe.wait_ge(u_ready, g.count(4, 4))
                elif p == 3 and to is None:
                    pe.wait_ge(sum_ready, g.count(4, 1))
                pe.matmul((to or ku_bank[p])[:, :], kt[:, p, :], u[:, p, :], start=True, stop=True).then_inc(ku_done, 1)

            def back(g):
                kernel_t(g)
                for p in range(PAIRS):
                    attend(g, p, [ps_k, *proj][p])

            def iteration(g, has_prev, has_next):
                first = not has_prev
                before = g.prev() if has_prev else None
                nxt = g.next() if has_next else None
                if has_next:
                    mix(nxt, 0)
                    mix(nxt, 1)
                project(g, 0, first)
                if has_next:
                    mix(nxt, 2)
                    mix(nxt, 3)
                project(g, 1, first)
                if has_prev:
                    kernel_t(before)
                project(g, 2, first)
                if has_prev:
                    for p in range(PAIRS):
                        attend(before, p, mixed=nxt)
                for j in range(3, 7):
                    project(g, j, first)
                    if first and j == 3:
                        pe.wait_ge(sq_summed, 3)
                        pe.wait_ge(norm_copied, 1)
                        pe.matmul(ps_k[:, 2:3], ones[:, :], ssq[:, 2:3], start=True, stop=True).then_inc(norm_done, 1)
                project(g, 7, first)
                if first:
                    pe.wait_ge(wt_lo, 3)
                values(g, 0)
                gram(g, first)
                values(g, 1)
                symmetrise(g)
                values(g, 2)
                spread(g, first)
                values(g, 3)

            pe.wait_ge(dve_const, 3)
            for p in range(PAIRS):
                mix(Group(0, 0), p, first=True)
            for s_n, s in enumerate(("lang", "grav")):
                pe.wait_ge(w_loaded[s], 16)
                for k in range(DC):
                    n = s_n * DC + k
                    if n >= 3:
                        pe.wait_ge(gw_copied, n - 2)
                    for e in range(DC):
                        mm = pe.matmul(proj[n % 3][:, 0:(k + 1) * P], w_raw[s][:, e, k * P:(k + 1) * P],
                                       w_raw[s][:, e, 0:(k + 1) * P], start=(e == 0), stop=(e == DC - 1))
                    mm.then_inc(gw_done, 1)
            pe.wait_ge(w_loaded["o"], 16)
            for c in range(DC):
                if c >= 2:
                    pe.wait_ge(wot_copied, c - 1)
                else:
                    pe.wait_ge(y_ready, c + 3)
                for e in range(DC):
                    mm = pe.transpose(front[c % 2][:, e * P:(e + 1) * P],
                                      w_raw["o"][:, e, c * P:(c + 1) * P], ident[:, :])
                mm.then_inc(wot_done, 1)
            pe.wait_ge(sq_summed, 2)
            pe.wait_ge(dve_const, 1)
            pe.matmul(ps_k[:, 0:2], ones[:, :], ssq[:, 0:2], start=True, stop=True).then_inc(norm_done, 1)
            pe.wait_ge(wot_copied, DC)
            pe.wait_ge(w_loaded["v"], 16)
            for k in range(DC):
                n = 2 * DC + k
                pe.wait_ge(gw_copied, n - 2)
                for v in range(DC):
                    mm = pe.matmul(proj[n % 3][:, :], w_raw["v"][:, v, k * P:(k + 1) * P],
                                   wo_t[:, v, :], start=(v == 0), stop=(v == DC - 1))
                mm.then_inc(gw_done, 1)
            pe.wait_ge(gw_copied, 3 * DC)
            pe.wait_ge(wt_lo, 2)
            run(pe, iteration, back)

        @block.scalar
        def _(act):
            def h_high(g, p):
                act.wait_ge(h_ready, g.count(4, p + 1))
                act.activation(h_hi[:, p, :], h[g.parity][:, p, :], ACT.Copy).then_inc(hhi_ready, 1)

            def transposes(g, first, last):
                for n in range(first, last):
                    p, part, part_t = n // 2, (h_hi, h_lo)[n % 2], (ht_hi, ht_lo)[n % 2]
                    act.dma_start_transpose(part_t[g.parity][:, :, p * P:(p + 1) * P],
                                            part[:, p, :]).then_inc(ht_loaded[g.parity], 16)

            def p_high(g, j, first):
                if j == 0 and not first:
                    act.wait_ge(gram_done, g.prev().count(1, 1))
                act.wait_ge(proj_done, g.count(12, j + 1))
                act.activation(p_hi[:, j % 4, :, j // 4, :], by_batch(proj[j % 3]),
                               ACT.Copy).then_inc(phi_ready, 1)

            def u_copy(g, p):
                act.wait_ge(proj_done, g.count(12, 9 + p))
                act.activation(u[:, p, :], proj[(8 + p) % 3][:, :], ACT.Copy).then_inc(u_ready, 1)

            def t_copy(g, first):
                act.wait_ge(gram_done, g.count(1, 1))
                if first:
                    act.wait_ge(t_scale_ready, 2)
                else:
                    act.wait_ge(s_ready, g.prev().count(1, 1))
                act.activation(t_sb[:, :], ps_t[:, :], ACT.Copy, scale=t_scale[:, 0:1]).then_inc(t_ready, 1)

            def exponent(g):
                act.wait_ge(d2_ready, g.count(2, 2))
                act.activation(e_sb[GR, :], w_sb[GR, :], ACT.Exp, scale=cexp[GR, 0:1]).then_inc(exp_ready, 1)

            def kt_copy(g):
                act.wait_ge(kt_done, g.count(1, 1))
                for q in range(2):
                    half = slice(q * N, (q + 1) * N)
                    act.activation(kt[half, :, half], ps_v[half, 0:PAIRS * N].rearrange("p (a n) -> p a n", a=PAIRS),
                                   ACT.Copy).then_inc(kt_ready, 1)

            def normalise(g, pairs):
                act.wait_ge(nmr2_ready, g.count(1, 1))
                for p in pairs:
                    act.activation(o[:, p, :], o[:, p, :], ACT.Identity, scale=rstd2[:, p:p + 1],
                                   bias=nmr2[:, p:p + 1]).then_inc(out_ready, 1)

            def m_high():
                act.wait_ge(scale_ready, 3)
                act.activation(m_hi[:, :, :].rearrange("p a b -> p (a b)"), m_f32, ACT.Copy,
                               scale=up[:, 2:3]).then_inc(wt_hi, 1)

            def back(g):
                kt_copy(g)
                normalise(g, (0, 1))

            def iteration(g, has_prev, has_next):
                first = not has_prev
                before = g.prev() if has_prev else None
                nxt = g.next() if has_next else None
                p_high(g, 0, first)
                p_high(g, 1, first)
                if has_prev:
                    kt_copy(before)
                p_high(g, 2, first)
                if has_next:
                    h_high(nxt, 0)
                    h_high(nxt, 1)
                    h_high(nxt, 2)
                p_high(g, 3, first)
                if has_next:
                    h_high(nxt, 3)
                    act.wait_ge(hlo_ready, nxt.count(4, 1))
                p_high(g, 4, first)
                if first:
                    m_high()
                if has_next:
                    transposes(nxt, 0, 1)
                p_high(g, 5, first)
                if has_next:
                    transposes(nxt, 1, 2)
                p_high(g, 6, first)
                if has_next:
                    act.wait_ge(hlo_ready, nxt.count(4, 4))
                p_high(g, 7, first)
                if has_next:
                    transposes(nxt, 2, 4)
                u_copy(g, 0)
                if has_next:
                    transposes(nxt, 4, 6)
                t_copy(g, first)
                if has_next:
                    transposes(nxt, 6, 7)
                u_copy(g, 1)
                if has_next:
                    transposes(nxt, 7, 8)
                if has_prev:
                    normalise(before, (0, 1))
                u_copy(g, 2)
                if has_prev:
                    normalise(before, (2,))
                exponent(g)
                if has_prev:
                    normalise(before, (3,))
                u_copy(g, 3)

            for p in range(PAIRS):
                h_high(Group(0, 0), p)
            act.wait_ge(small_loaded, 32)
            act.activation(gexp[:, :], gate_b[:, :], ACT.Exp, scale=-1.0).then_inc(act_const, 1)
            act.activation(sexp[:, :], lsig_b[:, :], ACT.Exp, scale=-2.0).then_inc(act_const, 1)
            for s_n, s in enumerate(("lang", "grav")):
                act.wait_ge(gw_copied, DC * (s_n + 1))
                act.activation(square[s_n][:, 0:NBLK * P], l_f32[s][:, :], ACT.Square,
                               accum_out=ssq[:, s_n:s_n + 1]).then_inc(sq_summed, 1)
            for c in range(DC):
                act.wait_ge(wot_done, c + 1)
                act.activation(wo_t[:, c, :], front[c % 2][:, :], ACT.Copy).then_inc(wot_copied, 1)
            act.wait_ge(hlo_ready, 4)
            transposes(Group(0, 0), 0, 8)
            for s_n, s in enumerate(("lang", "grav")):
                act.wait_ge(scale_ready, 1)
                act.activation(l_hi[s][:, :, :].rearrange("p a b -> p (a b)"), l_f32[s][:, :], ACT.Copy,
                               scale=up[:, s_n:s_n + 1]).then_inc(wt_hi, 1)
            act.wait_ge(gw_copied, 3 * DC)
            act.wait_ge(sq_summed, 2)
            act.activation(square[0][:, 0:DC * D], m_f32, ACT.Square,
                           accum_out=ssq[:, 2:3]).then_inc(sq_summed, 1)
            act.wait_ge(sq_summed, 3)
            run(act, iteration, back)

        @block.vector
        def _(dve):
            def add_bias(g, p):
                dve.wait_ge(l0_done, g.count(4, p + 1))
                dve.tensor_tensor(y[:, p, :], front[p % 2][:, :], bias_b[:, :], ALU.add).then_inc(y_ready, 1)

            def row_stats(g, p):
                dve.wait_ge(y_ready, g.count(4, p + 1))
                dve.bn_stats(stats1[:, p, :], y[:, p, :]).then_inc(stats1_ready, 1)

            def row_moments(g):
                for p in range(PAIRS):
                    dve.bn_aggr(mv1[:, p, :], stats1[:, p, :]).then_inc(mv1_ready, 1)

            def norm_rows(g, readers=None):
                dve.wait_ge(rstd1_ready, g.count(1, 1))
                for p in range(PAIRS):
                    if readers:
                        dve.wait_ge(sum_ready, readers.count(4, p + 1))
                    dve.tensor_scalar(h[g.parity][:, p, :], y[:, p, :], mv1[:, p, 0:1], rstd1[:, p:p + 1],
                                      ALU.subtract, ALU.mult).then_inc(h_ready, 1)

            def h_low(g, p):
                dve.wait_ge(hhi_ready, g.count(4, p + 1))
                dve.tensor_tensor(h_lo[:, p, :], h[g.parity][:, p, :], h_hi[:, p, :],
                                  ALU.subtract).then_inc(hlo_ready, 1)

            def p_low(g, j):
                dve.wait_ge(phi_ready, g.count(8, j + 1))
                dve.tensor_tensor(p_lo[:, j % 4, :, j // 4, :], by_batch(proj[j % 3]),
                                  p_hi[:, j % 4, :, j // 4, :], ALU.subtract).then_inc(plo_ready, 1)

            def diagonals(g):
                dve.wait_ge(tdiag_ready, g.count(1, 1))
                dve.reduce_sum(diag[:, :], by_batch(t_diag), X_AXIS).then_inc(diag_ready, 1)
                dve.wait_ge(diag_ready, g.count(1, 1))
                dve.tensor_scalar(nsq[L, :], diag[L, :], 2.0, EPS_NORM_SQ, ALU.mult, ALU.max).then_inc(nsq_ready, 1)
                dve.tensor_scalar(vec[GR, :], diag[GR, :], 2.0, None, ALU.mult).then_inc(nsq_ready, 1)

            def diagonal_matrices(g):
                dve.wait_ge(rinv_ready, g.count(1, 1))
                dve.wait_ge(nsq_ready, g.count(2, 2))
                dve.tensor_tensor(by_batch(v_diag), over_batches(eye2), over_columns(vec),
                                  ALU.mult).then_inc(v_ready, 1)

            def sums(g):
                dve.wait_ge(sym_done, g.count(1, 1))
                dve.tensor_tensor(s_sb[:, :], ps_t[:, :], t_sb[:, :], ALU.add).then_inc(s_ready, 1)

            def distances(g):
                dve.wait_ge(dj_done, g.count(1, 1))
                dve.wait_ge(s_ready, g.count(1, 1))
                dve.scalar_tensor_tensor(out=s_sb[GR, :], in0=s_sb[GR, :], scalar=-2.0, in1=ps_v[GR, :],
                                         op0=ALU.mult, op1=ALU.add).then_inc(d2_ready, 1)
                dve.tensor_tensor(by_batch(w_sb, 0, N), by_batch(ps_v, 0, N), over_batches(mask, 0, N),
                                  ALU.mult).then_inc(mr_ready, 1)
                dve.wait_ge(d2_ready, g.count(2, 1))
                dve.tensor_tensor(by_batch(w_sb, N, P), by_batch(s_sb, N, P), over_columns(vec, N, P),
                                  ALU.add).then_inc(d2_ready, 1)

            def similarities(g):
                dve.wait_ge(mr_ready, g.count(1, 1))
                dve.scalar_tensor_tensor(out=a_sb[L, :], in0=s_sb[L, :], scalar=0.0, in1=w_sb[L, :],
                                         op0=ALU.max, op1=ALU.mult).then_inc(a_ready, 1)

            def gravities(g):
                dve.wait_ge(exp_ready, g.count(1, 1))
                dve.scalar_tensor_tensor(out=by_batch(a_sb, N, P), in0=by_batch(e_sb, N, P), scalar=1.0,
                                         in1=over_batches(mask, N, P), op0=ALU.min,
                                         op1=ALU.mult).then_inc(a_ready, 1)

            def row_factors(g, between=()):
                steps = iter(between)

                def other():
                    step = next(steps, None)
                    if step:
                        step()

                dve.wait_ge(a_ready, g.count(2, 2))
                dve.reduce_sum(deg[:, :], by_batch(a_sb), X_AXIS).then_inc(deg_ready, 1)
                other()
                dve.wait_ge(deg_ready, g.count(5, 1))
                dve.wait_ge(rr_ready, g.count(1, 1))
                dve.tensor_tensor(degr[:, :], deg[:, :], rr[:, :], ALU.mult).then_inc(deg_ready, 1)
                other()
                dve.wait_ge(deg_ready, g.count(5, 2))
                dve.tensor_scalar(degm[:, :], degr[:, :], EPS_DEG, None, ALU.max).then_inc(deg_ready, 1)
                other()
                dve.wait_ge(deg_ready, g.count(5, 3))
                dve.reciprocal(dinv[:, :], degm[:, :]).then_inc(deg_ready, 1)
                other()
                dve.wait_ge(deg_ready, g.count(5, 4))
                dve.scalar_tensor_tensor(out=cfac[:, :], in0=dinv[:, :], scalar=wv_scale[:, 0:1], in1=rr[:, :],
                                         op0=ALU.mult, op1=ALU.mult).then_inc(deg_ready, 1)

            def scale_rows(g):
                dve.wait_ge(deg_ready, g.count(5, 5))
                dve.tensor_tensor(by_batch(ks_sb), by_batch(a_sb), over_columns(cfac), ALU.mult).then_inc(ks_ready, 1)

            def residual(g, p, first, source=None):
                dve.wait_ge(ku_done, g.count(4, p + 1))
                if p == 0 and not first:
                    dve.wait_ge(stored, g.prev().count(16, 16))
                dve.tensor_tensor(o[:, p, :], (source or ku_bank[p])[:, :], h[g.parity][:, p, :], ALU.add).then_inc(sum_ready, 1)

            def out_stats(g, p):
                dve.wait_ge(sum_ready, g.count(4, p + 1))
                dve.bn_stats(stats2[:, p, :], o[:, p, :]).then_inc(stats2_ready, 1)

            def out_moments(g):
                for p in range(PAIRS):
                    dve.bn_aggr(mv2[:, p, :], stats2[:, p, :]).then_inc(mv2_ready, 1)

            def out_shift(g):
                dve.wait_ge(rstd2_ready, g.count(1, 1))
                dve.scalar_tensor_tensor(out=nmr2[:, :], in0=mv2[:, :, 0], scalar=-1.0, in1=rstd2[:, :],
                                         op0=ALU.mult, op1=ALU.mult).then_inc(nmr2_ready, 1)

            def m_scale():
                dve.wait_ge(norm_done, 2)
                dve.tensor_scalar(ssq_all[:, 2:3], ps_k[:, 2:3], TINY, None, ALU.max).then_inc(norm_copied, 1)
                dve.wait_ge(norm_pow, 2)
                dve.tensor_scalar(up[:, 2:3], rnorm[:, 2:3], FP16_NORM, None, ALU.mult).then_inc(scale_ready, 1)
                dve.wait_ge(scale_ready, 3)
                dve.reciprocal(down[:, 2:3], up[:, 2:3]).then_inc(scale_ready, 1)
                dve.wait_ge(scale_ready, 4)
                dve.wait_ge(dve_const, 13)
                dve.tensor_tensor(wv_scale[:, :], wside[:, :], down[:, 2:3], ALU.mult).then_inc(scale_ready, 1)

            def m_low():
                dve.wait_ge(wt_hi, 3)
                dve.scalar_tensor_tensor(out=m_lo[:, :, :].rearrange("p a b -> p (a b)"), in0=m_f32,
                                         scalar=up[:, 2:3], in1=m_hi[:, :, :].rearrange("p a b -> p (a b)"),
                                         op0=ALU.mult, op1=ALU.subtract).then_inc(wt_lo, 1)

            def back(g):
                similarities(g)
                gravities(g)
                row_factors(g)
                scale_rows(g)
                for p in range(PAIRS):
                    residual(g, p, False, [ps_k, *proj][p])
                    if p:
                        out_stats(g, p - 1)
                out_stats(g, PAIRS - 1)
                dve.wait_ge(stats2_ready, g.count(4, 4))
                dve.tensor_copy(nsq[:, 0:1], stats2[:, 0, 0:1])
                out_moments(g)
                out_shift(g)
                dve.wait_ge(nmr2_ready, g.count(1, 1))
                for p in (2, 3):
                    dve.tensor_scalar(o[:, p, :], o[:, p, :], rstd2[:, p:p + 1], nmr2[:, p:p + 1],
                                      ALU.mult, ALU.add).then_inc(out_ready_dve, 1)

            def iteration(g, has_prev, has_next):
                first = not has_prev
                before = g.prev() if has_prev else None
                nxt = g.next() if has_next else None
                if has_prev:
                    similarities(before)
                    gravities(before)
                if has_next:
                    add_bias(nxt, 0)
                    add_bias(nxt, 1)
                stats01 = [lambda p=p: row_stats(nxt, p) for p in (0, 1)] if has_next else []
                if has_prev:
                    row_factors(before, stats01)
                    p_low(g, 0)
                    scale_rows(before)
                else:
                    for step in stats01:
                        step()
                    p_low(g, 0)
                if has_next:
                    for p in (2, 3):
                        add_bias(nxt, p)
                    for p in (2, 3):
                        row_stats(nxt, p)
                    dve.wait_ge(stats1_ready, nxt.count(4, 4))
                p_low(g, 1)
                if has_next:
                    row_moments(nxt)
                if has_prev:
                    residual(before, 0, False)
                    residual(before, 1, False)
                    out_stats(before, 0)
                    residual(before, 2, False)
                    out_stats(before, 1)
                    residual(before, 3, False)
                p_low(g, 2)
                if has_next:
                    norm_rows(nxt, before)
                    h_low(nxt, 0)
                    h_low(nxt, 1)
                p_low(g, 3)
                if has_next:
                    h_low(nxt, 2)
                p_low(g, 4)
                if first:
                    m_scale()
                if has_next:
                    h_low(nxt, 3)
                if has_prev:
                    out_stats(before, 2)
                p_low(g, 5)
                if has_prev:
                    out_stats(before, 3)
                if first:
                    m_low()
                if has_prev:
                    dve.wait_ge(stats2_ready, before.count(4, 4))
                p_low(g, 6)
                if has_prev:
                    out_moments(before)
                p_low(g, 7)
                if has_prev:
                    out_shift(before)
                diagonals(g)
                diagonal_matrices(g)
                sums(g)
                distances(g)

            dve.memset(ones[:, :], 1.0).then_inc(dve_const, 1)
            dve.memset(minus_half[:, :], -0.5).then_inc(half_ready, 1)
            dve.wait_ge(adj_loaded, 32)
            dve.tensor_tensor(adj_sq[:, :], adj2[:, :], adj2[:, :], ALU.mult).then_inc(dve_const, 1)
            dve.wait_ge(dve_const, 2)
            dve.wait_ge(pool_const, 10)
            dve.tensor_tensor(wmix[L, L], adj_sq[L, :], eye2[L, :], ALU.add)
            dve.tensor_tensor(wmix[GR, GR], adj_sq[GR, :], eye2[GR, :], ALU.add).then_inc(dve_const, 1)
            dve.tensor_scalar(not_eye[:, :], eye2[:, :], -1.0, 1.0, ALU.mult, ALU.add).then_inc(dve_const, 1)
            dve.wait_ge(dve_const, 4)
            dve.tensor_tensor(mask[:, :], adj2[:, :], not_eye[:, :], ALU.mult).then_inc(dve_const, 1)
            dve.tensor_copy(eye_l[:, :], ident[:, 0:N]).then_inc(dve_const, 1)
            dve.tensor_copy(eye_g[:, :], ident[:, N:P]).then_inc(dve_const, 1)
            dve.memset(rr[:, :], 1.0).then_inc(dve_const, 1)
            g0 = Group(0, 0)
            dve.wait_ge(bias_loaded, 16)
            for p in range(PAIRS):
                add_bias(g0, p)
            for p in range(PAIRS):
                row_stats(g0, p)
            dve.wait_ge(stats1_ready, 4)
            row_moments(g0)
            norm_rows(g0)
            for p in range(PAIRS):
                h_low(g0, p)
            for s_n, s in enumerate(("lang", "grav")):
                for k in range(DC):
                    n = s_n * DC + k
                    dve.wait_ge(gw_done, n + 1)
                    if k:
                        dve.tensor_copy(l_f32[s][:, blk(k, 0) * P:blk(k, k) * P], proj[n % 3][:, 0:k * P])
                    done = dve.tensor_scalar(l_f32[s][:, blk(k, k) * P:(blk(k, k) + 1) * P],
                                             proj[n % 3][:, k * P:(k + 1) * P], 0.5, None, ALU.mult)
                    done.then_inc(gw_copied, 1)
            dve.wait_ge(act_const, 2)
            dve.tensor_scalar(gexp1[:, :], gexp[:, :], 1.0, None, ALU.add).then_inc(dve_const, 1)
            dve.tensor_scalar(cexp[:, :], sexp[:, :], -0.5, None, ALU.mult).then_inc(dve_const, 1)
            dve.wait_ge(dve_const, 10)
            dve.reciprocal(wgate[:, :], gexp1[:, :]).then_inc(dve_const, 1)
            dve.wait_ge(dve_const, 11)
            dve.tensor_copy(wside[L, :], wgate[L, :]).then_inc(dve_const, 1)
            dve.tensor_scalar(wside[GR, :], wgate[GR, :], -1.0, 1.0, ALU.mult, ALU.add).then_inc(dve_const, 1)
            dve.wait_ge(norm_done, 1)
            dve.tensor_scalar(ssq_all[:, 0:2], ps_k[:, 0:2], TINY, None, ALU.max).then_inc(norm_copied, 1)
            dve.wait_ge(norm_pow, 1)
            dve.tensor_scalar(up[:, 0:2], rnorm[:, 0:2], FP16_NORM, None, ALU.mult).then_inc(scale_ready, 1)
            dve.wait_ge(scale_ready, 1)
            dve.reciprocal(down[:, 0:2], up[:, 0:2]).then_inc(scale_ready, 1)
            dve.wait_ge(scale_ready, 2)
            dve.tensor_copy(t_scale[L, :], down[L, 0:1]).then_inc(t_scale_ready, 1)
            dve.tensor_copy(t_scale[GR, :], down[GR, 1:2]).then_inc(t_scale_ready, 1)
            for k in range(DC):
                n = 2 * DC + k
                dve.wait_ge(gw_done, n + 1)
                dve.tensor_copy(m_f32[:, k * D:(k + 1) * D], proj[n % 3][:, :]).then_inc(gw_copied, 1)
                if k < 2:
                    s = ("lang", "grav")[k]
                    dve.wait_ge(wt_hi, k + 1)
                    dve.scalar_tensor_tensor(out=l_lo[s][:, :, :].rearrange("p a b -> p (a b)"), in0=l_f32[s][:, :],
                                             scalar=up[:, k:k + 1],
                                             in1=l_hi[s][:, :, :].rearrange("p a b -> p (a b)"),
                                             op0=ALU.mult, op1=ALU.subtract).then_inc(wt_lo, 1)
            run(dve, iteration, back)

        @block.gpsimd
        def _(pool):
            def inverse_std(g, mv_ready, mv, ve_ready, ve, rstd_ready, rstd):
                pool.wait_ge(mv_ready, g.count(4, 4))
                pool.tensor_tensor(ve[:, :], mv[:, :, 1], eps_ln[:, :], ALU.add).then_inc(ve_ready, 1)
                pool.wait_ge(ve_ready, g.count(1, 1))
                pool.tensor_tensor(rstd[:, :], ve[:, :], minus_half[:, 0:PAIRS], ALU.pow).then_inc(rstd_ready, 1)

            def ln1(g):
                inverse_std(g, mv1_ready, mv1, ve1_ready, ve1, rstd1_ready, rstd1)

            def ln2(g):
                inverse_std(g, mv2_ready, mv2, ve2_ready, ve2, rstd2_ready, rstd2)

            def t_diagonal(g):
                pool.wait_ge(t_ready, g.count(1, 1))
                pool.tensor_tensor(by_batch(t_diag), by_batch(t_sb), over_batches(eye2),
                                   ALU.mult).then_inc(tdiag_ready, 1)

            def inverse_norm(g):
                pool.wait_ge(nsq_ready, g.count(2, 1))
                pool.tensor_tensor(vec[L, :], nsq[L, :], minus_half[L, :], ALU.pow).then_inc(rinv_ready, 1)
                pool.tensor_tensor(rr[L, :], nsq[L, :], minus_half[L, :], ALU.pow).then_inc(rr_ready, 1)

            def iteration(g, has_prev, has_next):
                if has_next:
                    ln1(g.next())
                if not has_prev:
                    pool.wait_ge(norm_copied, 2)
                    pool.tensor_tensor(rnorm[:, 2:3], ssq_all[:, 2:3], minus_half[:, 2:3], ALU.pow).then_inc(norm_pow, 1)
                if has_prev:
                    ln2(g.prev())
                t_diagonal(g)
                inverse_norm(g)

            pool.memset(ident[:, :], 0.0).then_inc(pool_const, 1)
            pool.wait_ge(pool_const, 1)
            pool.affine_select(out=ident[:, :], in_=ident[:, :], compare_op=ALU.not_equal, fill=1.0, base=0,
                               pattern=[[-1, P]], channel_multiplier=1).then_inc(pool_const, 1)
            pool.wait_ge(pool_const, 2)
            pool.tensor_copy(eye2[L, :], ident[L, 0:N]).then_inc(pool_const, 1)
            pool.wait_ge(pool_const, 3)
            pool.tensor_copy(eye2[GR, :], ident[GR, N:P]).then_inc(pool_const, 1)
            pool.wait_ge(pool_const, 4)
            pool.memset(ones_lg[:, :], 0.0).then_inc(pool_const, 1)
            pool.wait_ge(pool_const, 5)
            pool.memset(ones_lg[L, 0:N], 1.0).then_inc(pool_const, 1)
            pool.wait_ge(pool_const, 6)
            pool.memset(ones_lg[GR, N:P], 1.0).then_inc(pool_const, 1)
            pool.wait_ge(pool_const, 7)
            pool.memset(kt[:, :, :], 0.0).then_inc(pool_const, 1)
            pool.memset(eps_ln[:, :], EPS_LN).then_inc(pool_const, 1)
            pool.memset(wmix[:, :], 0.0).then_inc(pool_const, 1)
            pool.wait_ge(pool_const, 10)
            pool.wait_ge(half_ready, 1)
            ln1(Group(0, 0))
            pool.wait_ge(norm_copied, 1)
            pool.tensor_tensor(rnorm[:, 0:2], ssq_all[:, 0:2], minus_half[:, 0:2], ALU.pow).then_inc(norm_pow, 1)
            run(pool, iteration, ln2)


_INS = ["x", "adj", "L0_gnn_bias", "L1_gnn_W_lang", "L1_gnn_W_grav", "L1_gnn_W_V", "L1_gnn_W_O",
        "L1_gnn_gate_logit", "L1_gnn_log_sigma"]


def kernel(**inputs):
    import numpy as np
    import concourse.bacc as bacc
    from concourse.bass_utils import run_bass_kernel_spmd

    nc = bacc.Bacc("TRN2", target_bir_lowering=False, num_devices=1)
    arrays, args = {}, []
    for name in _INS:
        a = np.ascontiguousarray(inputs[name])
        arrays[f"in_{name}"] = a
        args.append(nc.dram_tensor(f"in_{name}", a.shape, mybir.dt.from_np(a.dtype), kind="ExternalInput").ap())
    shape = inputs["x"].shape
    out = nc.dram_tensor("out", shape, F32, kind="ExternalOutput").ap()
    resnorm_graph_kernel(nc, *args, out)
    r = run_bass_kernel_spmd(nc, [arrays], core_ids=[0])
    return r.results[0]["out"]
```

```python
from contextlib import ExitStack

import concourse.bass as bass
from concourse import mybir

F32 = mybir.dt.float32
F16 = mybir.dt.float16
ALU = mybir.AluOpType
ACT = mybir.ActivationFunctionType
X_AXIS = mybir.AxisListType.X

P = 128
EPS_LN = 1e-5
EPS_DEG = 1e-8
EPS_NORM_SQ = 1e-16
TINY = 1e-30
FP16_NORM = 2048.0
WARM_START = 10


class Group:

    def __init__(self, half, parity):
        self.half, self.parity = half, parity

    def next(self):
        return Group(self.half + self.parity, 1 - self.parity)

    def prev(self):
        return Group(self.half - 1 + self.parity, 1 - self.parity)

    def count(self, per_group, n):
        return self.half * (2 * per_group) + (per_group * self.parity + n)


def resnorm_graph_kernel(nc, x, adj, bias, w_lang, w_grav, w_v, w_o, gate, log_sigma, out):
    B, N, D = x.shape
    DC = D // P
    GB = 8
    PAIRS = GB * N // P
    ROWS = GB * N
    G = B // GB
    NBLK = DC * (DC + 1) // 2
    g_last_out = PAIRS * (G - 1)
    assert N == 64 and D == 512 and G % 2 == 0 and ROWS == 512

    def blk(k, c):
        return k * (k + 1) // 2 + c

    x_dram = x.rearrange("(g p q) n d -> g (q n) p d", g=G, p=PAIRS, q=2)
    out_dram = out.rearrange("(g p q) n d -> g (q n) p d", g=G, p=PAIRS, q=2)

    ctx = ExitStack()
    with ctx:
        def sb(name, shape, dt=F32):
            return ctx.enter_context(nc.sbuf_tensor(name, shape, dt))

        def bank(name):
            return ctx.enter_context(nc.psum_tensor(name, [P, 512], F32))

        def sem(name):
            return ctx.enter_context(nc.semaphore(name))

        x_in = [sb(f"x_in{i}", [P, PAIRS, D]) for i in range(2)]
        y = sb("y", [P, PAIRS, D])
        h = [sb(f"h{i}", [P, PAIRS, D]) for i in range(2)]
        h_hi = sb("h_hi", [P, PAIRS, D], F16)
        h_lo = sb("h_lo", [P, PAIRS, D], F16)
        ht_hi = [sb(f"ht_hi{i}", [P, DC, ROWS], F16) for i in range(2)]
        ht_lo = [sb(f"ht_lo{i}", [P, DC, ROWS], F16) for i in range(2)]
        p_hi = sb("p_hi", [P, DC, GB, 2, N], F16)
        p_lo = sb("p_lo", [P, DC, GB, 2, N], F16)
        u = sb("u", [P, PAIRS, D])
        o = sb("o", [P, PAIRS, D])
        t_sb = sb("t_sb", [P, ROWS])
        t_diag = sb("t_diag", [P, ROWS])
        v_diag = sb("v_diag", [P, ROWS])
        s_sb = sb("s_sb", [P, ROWS])
        w_sb = sb("w_sb", [P, ROWS])
        e_sb = sb("e_sb", [P, ROWS])
        a_sb = sb("a_sb", [P, ROWS])
        ks_sb = sb("ks_sb", [P, ROWS])
        kt = sb("kt", [P, PAIRS, P])
        stats1 = sb("stats1", [P, PAIRS, 6])
        mv1 = sb("mv1", [P, PAIRS, 2])
        ve1 = sb("ve1", [P, PAIRS])
        rstd1 = sb("rstd1", [P, PAIRS])
        stats2 = sb("stats2", [P, PAIRS, 6])
        mv2 = sb("mv2", [P, PAIRS, 2])
        ve2 = sb("ve2", [P, PAIRS])
        rstd2 = sb("rstd2", [P, PAIRS])
        nmr2 = sb("nmr2", [P, PAIRS])
        hold = sb("hold", [P, 1])
        diag = sb("diag", [P, GB])
        nsq = sb("nsq", [P, GB])
        vec = sb("vec", [P, GB])
        rr = sb("rr", [P, GB])
        deg = sb("deg", [P, GB])
        degr = sb("degr", [P, GB])
        degm = sb("degm", [P, GB])
        dinv = sb("dinv", [P, GB])
        cfac = sb("cfac", [P, GB])
        w_raw = {n: sb(f"w_raw_{n}", [P, DC, D]) for n in ("lang", "grav")}
        w_raw["v"] = u
        w_raw["o"] = o
        wo_t = sb("wo_t", [P, DC, D])
        l_f32 = {"lang": sb("l_lang_f32", [P, NBLK * P]), "grav": sb("l_grav_f32", [P, NBLK * P])}
        m_f32 = sb("m_f32", [P, DC, D])
        square = [t[:, :, :, :, :].bitcast(F32).rearrange("p c b s n -> p (c b s n)") for t in (p_hi, p_lo)]
        l_hi = {s: sb(f"l_{s}_hi", [P, NBLK, P], F16) for s in ("lang", "grav")}
        l_lo = {s: sb(f"l_{s}_lo", [P, NBLK, P], F16) for s in ("lang", "grav")}
        m_hi = sb("m_hi", [P, DC, D], F16)
        m_lo = sb("m_lo", [P, DC, D], F16)
        ident = sb("ident", [P, P])
        ones = sb("ones", [P, P])
        ones_lg = sb("ones_lg", [P, P])
        eye2 = sb("eye2", [P, N])
        eye_g = sb("eye_g", [P, N])
        eye_l = sb("eye_l", [P, N])
        adj2 = sb("adj2", [P, N])
        adj_sq = sb("adj_sq", [P, N])
        wmix = sb("wmix", [P, P])
        not_eye = sb("not_eye", [P, N])
        mask = sb("mask", [P, N])
        bias_b = sb("bias_b", [P, D])
        gate_b = sb("gate_b", [P, 1])
        lsig_b = sb("lsig_b", [P, 1])
        gexp = sb("gexp", [P, 1])
        gexp1 = sb("gexp1", [P, 1])
        wgate = sb("wgate", [P, 1])
        wside = sb("wside", [P, 1])
        sexp = sb("sexp", [P, 1])
        cexp = sb("cexp", [P, 1])
        minus_half = sb("minus_half", [P, GB])
        eps_ln = sb("eps_ln", [P, PAIRS])
        ssq = sb("ssq", [P, 2 + DC])
        ssq_all = sb("ssq_all", [P, 3])
        rnorm = sb("rnorm", [P, 3])
        up = sb("up", [P, 3])
        down = sb("down", [P, 3])
        t_scale = sb("t_scale", [P, 1])
        wv_scale = sb("wv_scale", [P, 1])

        front = [bank(f"front{i}") for i in range(2)]
        proj = [bank(f"proj{i}") for i in range(3)]
        ps_t = bank("ps_t")
        ps_v = bank("ps_v")
        ps_k = bank("ps_k")
        ku_bank = [ps_k, *front, ps_k]
        last_ku_bank = [ps_k, *front, proj[0]]
        weight_bank = [*proj, ps_t]

        v_loaded = sem("v_loaded")
        w_rows_loaded = {n: [sem(f"w_{n}{e}_loaded") for e in range(DC)] for n in ("lang", "grav")}
        adj_loaded = sem("adj_loaded")
        bias_loaded = sem("bias_loaded")
        small_loaded = sem("small_loaded")
        x_loaded = [sem(f"x{i}_loaded") for i in range(2)]
        pool_const = sem("pool_const")
        dve_const = sem("dve_const")
        half_ready = sem("half_ready")
        gw_done = sem("gw_done")
        l_copied = sem("l_copied")
        g_copied = sem("g_copied")
        m_copied = sem("m_copied")
        wot_done = sem("wot_done")
        wot_copied = sem("wot_copied")
        act_const = sem("act_const")
        sq_summed = sem("sq_summed")
        norm_done = sem("norm_done")
        norm_copied = sem("norm_copied")
        norm_pow = sem("norm_pow")
        scale_ready = sem("scale_ready")
        t_scale_ready = sem("t_scale_ready")
        wt_hi = sem("wt_hi")
        wt_lo = sem("wt_lo")
        l0_done = sem("l0_done")
        y_ready = sem("y_ready")
        stats1_ready = sem("stats1_ready")
        mv1_ready = sem("mv1_ready")
        ve1_ready = sem("ve1_ready")
        rstd1_ready = sem("rstd1_ready")
        h_ready = sem("h_ready")
        hhi_ready = sem("hhi_ready")
        hlo_ready = sem("hlo_ready")
        hlo_ready_pool = sem("hlo_ready_pool")
        ht_loaded = [sem(f"ht{i}_loaded") for i in range(2)]
        proj_done = sem("proj_done")
        phi_ready = sem("phi_ready")
        plo_ready = sem("plo_ready")
        u_ready = sem("u_ready")
        gram_done = sem("gram_done")
        t_ready = sem("t_ready")
        tdiag_ready = sem("tdiag_ready")
        diag_ready = sem("diag_ready")
        nsq_ready = sem("nsq_ready")
        rinv_ready = sem("rinv_ready")
        rr_ready = sem("rr_ready")
        v_ready = sem("v_ready")
        sym_done = sem("sym_done")
        dj_done = sem("dj_done")
        s_ready = sem("s_ready")
        d2_ready = sem("d2_ready")
        mr_ready = sem("mr_ready")
        exp_ready = sem("exp_ready")
        a_ready = sem("a_ready")
        deg_ready = sem("deg_ready")
        ks_ready = sem("ks_ready")
        kt_done = sem("kt_done")
        kt_ready = sem("kt_ready")
        ku_done = sem("ku_done")
        sum_ready = sem("sum_ready")
        stats2_ready = sem("stats2_ready")
        mv2_ready = sem("mv2_ready")
        ve2_ready = sem("ve2_ready")
        rstd2_ready = sem("rstd2_ready")
        nmr2_ready = sem("nmr2_ready")
        out_ready = sem("out_ready")
        out_ready_dve = sem("out_ready_dve")
        o_moved = sem("o_moved")

        def by_batch(tile, lo=0, hi=P):
            return tile[lo:hi, :].rearrange("p (b n) -> p b n", b=GB)

        def over_columns(small, lo=0, hi=P):
            return small[lo:hi, :].unsqueeze(2).to_broadcast([hi - lo, GB, N])

        def over_batches(square_, lo=0, hi=P):
            return square_[lo:hi, :].unsqueeze(1).to_broadcast([hi - lo, GB, N])

        L, GR = slice(0, N), slice(N, P)

        block = ctx.enter_context(nc.Block())

        @block.sync
        def _(sp):
            def load(g):
                sp.dma_start(x_in[g.parity][:, :, :], x_dram[g.half * 2 + g.parity]).then_inc(x_loaded[g.parity], 16)

            def store(g):
                sp.wait_ge(out_ready, g.count(4, 4))
                sp.dma_start(out_dram[g.half * 2 + g.parity], o[:, :, :]).then_inc(o_moved, 16)

            def reload(g):
                sp.wait_ge(l0_done, g.count(4, 4))
                load(Group(g.half + 1, g.parity))

            view = {n: w.rearrange("(c p) d -> p c d", p=P)
                    for n, w in (("lang", w_lang), ("grav", w_grav), ("v", w_v), ("o", w_o))}
            sp.dma_start(adj2[0:N, :], adj).then_inc(adj_loaded, 16)
            sp.dma_start(adj2[N:P, :], adj).then_inc(adj_loaded, 16)
            for n in ("lang", "o", "grav", "v"):
                if n in ("o", "v"):
                    sp.dma_start(w_raw[n][:, :, :], view[n]).then_inc(o_moved if n == "o" else v_loaded, 16)
                else:
                    for e in range(DC):
                        sp.dma_start(w_raw[n][:, e, :], view[n][:, e, :]).then_inc(w_rows_loaded[n][e], 16)
                if n == "lang":
                    load(Group(0, 0))
                    sp.dma_start(bias_b[:, :], bias.unsqueeze(0).to_broadcast([P, D])).then_inc(bias_loaded, 16)
            sp.dma_start(gate_b[:, :], gate.unsqueeze(0).to_broadcast([P, 1])).then_inc(small_loaded, 16)
            sp.dma_start(lsig_b[:, :], log_sigma.unsqueeze(0).to_broadcast([P, 1])).then_inc(small_loaded, 16)
            load(Group(0, 1))
            reload(Group(0, 0))
            with sp.Fori(0, G // 2 - 2) as i:
                reload(Group(i, 1))
                store(Group(i, 0))
                reload(Group(i + 1, 0))
                store(Group(i, 1))
            last = G // 2 - 2
            reload(Group(last, 1))
            for g in (Group(last, 0), Group(last, 1), Group(last + 1, 0)):
                store(g)
            end = Group(last + 1, 1)
            for p in range(PAIRS):
                if p < 3:
                    sp.wait_ge(out_ready, g_last_out + p + 1)
                else:
                    sp.wait_ge(out_ready_dve, 1)
                sp.dma_start(out_dram[2 * end.half + end.parity][:, p, :], o[:, p, :]).then_inc(o_moved, 16)
            sp.wait_ge(o_moved, 16 + 16 * (G - 1 + PAIRS))

        def run(engine, iteration, back):
            iteration(Group(0, 0), has_prev=False, has_next=True)
            with engine.Fori(0, G // 2 - 1) as i:
                iteration(Group(i, 1), has_prev=True, has_next=True)
                iteration(Group(i + 1, 0), has_prev=True, has_next=True)
            iteration(Group(G // 2 - 1, 1), has_prev=True, has_next=False)
            back(Group(G // 2 - 1, 1))

        @block.tensor
        def _(pe):
            def keep_warm(products):
                for _ in range(products):
                    pe.matmul(ps_k[:, 0:P], ones[:, :], ones[:, :], start=True, stop=True)

            def mix(g, p, first=False):
                if p == 0:
                    pe.wait_ge(x_loaded[g.parity], g.half * 16 + 16)
                if p >= 2:
                    pe.wait_ge(y_ready, g.count(4, p - 1))
                elif not first:
                    pe.wait_ge(h_ready, g.prev().count(4, 1))
                pe.matmul(front[p % 2][:, :], wmix[:, :], x_in[g.parity][:, p, :],
                          start=True, stop=True).then_inc(l0_done, 1)

            def project(g, j, first):
                c, s = j % 4, ("lang", "grav")[j // 4]
                if j == 0:
                    pe.wait_ge(ht_loaded[g.parity], g.half * 128 + 128)
                    if first:
                        pe.wait_ge(wt_lo, 2)
                if j < 3:
                    if first:
                        pe.wait_ge(m_copied, j + 1)
                    else:
                        pe.wait_ge(u_ready, g.prev().count(4, j + 2))
                else:
                    pe.wait_ge(plo_ready, g.count(8, j - 2))
                passes = [(k, a, b) for k in range(c, DC)
                          for a, b in ((l_hi, ht_hi), (l_hi, ht_lo), (l_lo, ht_hi))]
                for n, (k, a, b) in enumerate(passes):
                    mm = pe.matmul(proj[j % 3][:, :], a[s][:, blk(k, c), :], b[g.parity][:, k, :],
                                   start=(n == 0), stop=(n == len(passes) - 1))
                mm.then_inc(proj_done, 1)

            def values(g, p, first=False):
                j = 8 + p
                if j < 11:
                    pe.wait_ge(plo_ready, g.count(8, j - 2))
                else:
                    pe.wait_ge(u_ready, g.count(4, 1))
                passes = [(k, a, b) for k in range(DC)
                          for a, b in ((ht_hi, m_hi), (ht_hi, m_lo), (ht_lo, m_hi))]
                for n, (k, a, b) in enumerate(passes):
                    if first and p == 0 and n % 3 == 0:
                        pe.wait_ge(wt_lo, 2 + k + 1)
                    mm = pe.matmul(proj[j % 3][:, :], a[g.parity][:, k, p * P:(p + 1) * P], b[:, k, :],
                                   start=(n == 0), stop=(n == len(passes) - 1))
                mm.then_inc(proj_done, 1)

            def gram(g, first):
                pe.wait_ge(phi_ready, g.count(8, 8))
                pe.wait_ge(plo_ready, g.count(8, 8))
                if not first:
                    pe.wait_ge(s_ready, g.prev().count(1, 1))
                passes = [(c, a, t) for c in range(DC)
                          for a, t in ((p_hi, ht_hi), (p_hi, ht_lo), (p_lo, ht_hi))]
                for b in range(GB):
                    for n, (c, a, t) in enumerate(passes):
                        mm = pe.matmul(ps_t[:, b * N:(b + 1) * N],
                                       a[:, c, b, :, :].rearrange("p s n -> p (s n)"),
                                       t[g.parity][:, c, b * N:(b + 1) * N],
                                       start=(n == 0), stop=(n == len(passes) - 1))
                mm.then_inc(gram_done, 1)

            def symmetrise(g):
                pe.wait_ge(t_ready, g.count(1, 1))
                for b in range(GB):
                    for half, eye in ((L, eye_l), (GR, eye_g)):
                        mm = pe.matmul(ps_t[half, b * N:(b + 1) * N], t_sb[:, b * N:(b + 1) * N],
                                       eye[:, :], start=True, stop=True)
                mm.then_inc(sym_done, 1)

            def spread(g, first):
                pe.wait_ge(v_ready, g.count(1, 1))
                if not first:
                    pe.wait_ge(kt_ready, g.prev().count(2, 2))
                pe.matmul(ps_v[:, :], ones_lg[:, :], v_diag[:, :], start=True, stop=True).then_inc(dj_done, 1)

            def kernel_t(g):
                pe.wait_ge(ks_ready, g.count(1, 1))
                for b in range(GB):
                    p, q = b // 2, b % 2
                    mm = pe.matmul(ps_v[q * N:(q + 1) * N, p * N:(p + 1) * N],
                                   ks_sb[:, b * N:(b + 1) * N], eye2[:, :], start=True, stop=True)
                mm.then_inc(kt_done, 1)

            def attend(g, p, mixed):
                if mixed and p in (1, 2):
                    pe.wait_ge(y_ready, mixed.count(4, p + 2))
                if p == 0:
                    pe.wait_ge(kt_ready, g.count(2, 2))
                    pe.wait_ge(u_ready, g.count(4, 4))
                elif p == 3:
                    pe.wait_ge(sum_ready, g.count(4, 1))
                pe.matmul(ku_bank[p][:, :], kt[:, p, :], u[:, p, :], start=True, stop=True).then_inc(ku_done, 1)

            def last_residual(g, p):
                if p < 2:
                    pe.wait_ge(sum_ready, g.prev().count(4, (4, 2)[p]))
                elif p == 2:
                    pe.wait_ge(sum_ready, g.prev().count(4, 3))
                pe.matmul(last_ku_bank[p][:, :], ident[:, :], h[g.parity][:, p, :], start=True, stop=False)

            def back(g):
                kernel_t(g)
                pe.wait_ge(kt_ready, g.count(2, 2))
                pe.wait_ge(u_ready, g.count(4, 4))
                for p in range(PAIRS):
                    pe.matmul(last_ku_bank[p][:, :], kt[:, p, :], u[:, p, :], start=(p == 3), stop=True).then_inc(ku_done, 1)

            def iteration(g, has_prev, has_next):
                first = not has_prev
                before = g.prev() if has_prev else None
                nxt = g.next() if has_next else None
                if has_next:
                    mix(nxt, 0)
                    mix(nxt, 1)
                if first:
                    pe.wait_ge(sq_summed, 2 + DC)
                    pe.wait_ge(norm_copied, 1)
                    for k in range(DC):
                        mm = pe.matmul(ps_k[:, 2:3], ones[:, :], ssq[:, 2 + k:3 + k], start=(k == 0), stop=(k == DC - 1))
                    mm.then_inc(norm_done, 1)
                project(g, 0, first)
                if has_next:
                    mix(nxt, 2)
                    mix(nxt, 3)
                project(g, 1, first)
                if has_prev:
                    kernel_t(before)
                project(g, 2, first)
                if has_prev:
                    for p in range(PAIRS):
                        attend(before, p, nxt)
                for j in range(3, 7):
                    project(g, j, first)
                project(g, 7, first)
                if has_next:
                    values(g, 0, first)
                    gram(g, first)
                    values(g, 1)
                    symmetrise(g)
                    values(g, 2)
                    spread(g, first)
                    values(g, 3)
                else:
                    last_residual(g, 0)
                    last_residual(g, 1)
                    gram(g, first)
                    values(g, 0)
                    symmetrise(g)
                    values(g, 1)
                    spread(g, first)
                    values(g, 2)
                    values(g, 3)
                    last_residual(g, 2)

            def gram_of(s):
                for e in range(DC):
                    pe.wait_ge(w_rows_loaded[s][e], 16)
                    for k in range(DC):
                        mm = pe.matmul(weight_bank[k][:, 0:(k + 1) * P], w_raw[s][:, e, k * P:(k + 1) * P],
                                       w_raw[s][:, e, 0:(k + 1) * P], start=(e == 0), stop=(e == DC - 1))
                        if e == DC - 1:
                            mm.then_inc(gw_done, 1)

            pe.wait_ge(dve_const, 1)
            keep_warm(WARM_START)
            gram_of("lang")
            pe.wait_ge(dve_const, 3)
            for p in range(PAIRS):
                mix(Group(0, 0), p, first=True)
            pe.wait_ge(o_moved, 16)
            for c in range(DC):
                if c >= 2:
                    pe.wait_ge(wot_copied, c - 1)
                else:
                    pe.wait_ge(y_ready, c + 3)
                for e in range(DC):
                    mm = pe.transpose(front[c % 2][:, e * P:(e + 1) * P],
                                      w_raw["o"][:, e, c * P:(c + 1) * P], ident[:, :])
                mm.then_inc(wot_done, 1)
            pe.wait_ge(l_copied, DC)
            gram_of("grav")
            pe.wait_ge(wot_copied, DC)
            pe.wait_ge(v_loaded, 16)
            for k in range(DC):
                pe.wait_ge(g_copied, k + 1)
                for v in range(DC):
                    mm = pe.matmul(weight_bank[k][:, :], w_raw["v"][:, v, k * P:(k + 1) * P],
                                   wo_t[:, v, :], start=(v == 0), stop=(v == DC - 1))
                mm.then_inc(gw_done, 1)
                if k == 0:
                    pe.wait_ge(sq_summed, 2)
                    pe.matmul(ps_k[:, 0:2], ones[:, :], ssq[:, 0:2], start=True, stop=True).then_inc(norm_done, 1)
            run(pe, iteration, back)

        @block.scalar
        def _(act):
            def h_high(g, p):
                act.wait_ge(h_ready, g.count(4, p + 1))
                act.activation(h_hi[:, p, :], h[g.parity][:, p, :], ACT.Copy).then_inc(hhi_ready, 1)

            def transposes(g, first, last):
                for n in range(first, last):
                    p, part, part_t = n // 2, (h_hi, h_lo)[n % 2], (ht_hi, ht_lo)[n % 2]
                    act.dma_start_transpose(part_t[g.parity][:, :, p * P:(p + 1) * P],
                                            part[:, p, :]).then_inc(ht_loaded[g.parity], 16)

            def p_high(g, j, first):
                if j == 0 and not first:
                    act.wait_ge(gram_done, g.prev().count(1, 1))
                act.wait_ge(proj_done, g.count(12, j + 1))
                act.activation(p_hi[:, j % 4, :, j // 4, :], by_batch(proj[j % 3]),
                               ACT.Copy).then_inc(phi_ready, 1)

            def u_copy(g, p):
                act.wait_ge(proj_done, g.count(12, 9 + p))
                act.activation(u[:, p, :], proj[(8 + p) % 3][:, :], ACT.Copy).then_inc(u_ready, 1)

            def t_copy(g, first):
                act.wait_ge(gram_done, g.count(1, 1))
                if first:
                    act.wait_ge(t_scale_ready, 2)
                else:
                    act.wait_ge(s_ready, g.prev().count(1, 1))
                act.activation(t_sb[:, :], ps_t[:, :], ACT.Copy, scale=t_scale[:, 0:1]).then_inc(t_ready, 1)

            def exponent(g):
                act.wait_ge(d2_ready, g.count(2, 2))
                act.activation(e_sb[GR, :], w_sb[GR, :], ACT.Exp, scale=cexp[GR, 0:1]).then_inc(exp_ready, 1)

            def kt_copy(g):
                act.wait_ge(kt_done, g.count(1, 1))
                for q in range(2):
                    half = slice(q * N, (q + 1) * N)
                    act.activation(kt[half, :, half], ps_v[half, 0:PAIRS * N].rearrange("p (a n) -> p a n", a=PAIRS),
                                   ACT.Copy).then_inc(kt_ready, 1)

            def last_normalise(g, p):
                act.wait_ge(o_moved, g.prev().count(16, 32))
                act.wait_ge(nmr2_ready, g.count(1, 1 + p // 2))
                act.activation(o[:, p, :], last_ku_bank[p][:, :], ACT.Identity, scale=rstd2[:, p:p + 1],
                               bias=nmr2[:, p:p + 1]).then_inc(out_ready, 1)

            def normalise(g, pairs):
                act.wait_ge(nmr2_ready, g.count(1, 1))
                for p in pairs:
                    act.activation(o[:, p, :], o[:, p, :], ACT.Identity, scale=rstd2[:, p:p + 1],
                                   bias=nmr2[:, p:p + 1]).then_inc(out_ready, 1)

            def m_high(half):
                act.wait_ge(scale_ready, 3)
                ks = slice(2 * half, 2 * half + 2)
                act.activation(m_hi[:, ks, :], m_f32[:, ks, :], ACT.Copy, scale=up[:, 2:3]).then_inc(wt_hi, 1)

            def back(g):
                kt_copy(g)
                for p in range(3):
                    last_normalise(g, p)

            def iteration(g, has_prev, has_next):
                first = not has_prev
                before = g.prev() if has_prev else None
                nxt = g.next() if has_next else None
                if first:
                    m_high(0)
                p_high(g, 0, first)
                if first:
                    m_high(1)
                p_high(g, 1, first)
                if has_prev:
                    kt_copy(before)
                p_high(g, 2, first)
                if has_next:
                    h_high(nxt, 0)
                    h_high(nxt, 1)
                    h_high(nxt, 2)
                p_high(g, 3, first)
                if has_next:
                    h_high(nxt, 3)
                    act.wait_ge(hlo_ready, nxt.count(2, 3))
                p_high(g, 4, first)
                if has_next:
                    transposes(nxt, 0, 1)
                p_high(g, 5, first)
                if has_next:
                    transposes(nxt, 1, 2)
                p_high(g, 6, first)
                if has_next:
                    act.wait_ge(hlo_ready, nxt.count(2, 4))
                p_high(g, 7, first)
                if has_next:
                    transposes(nxt, 2, 4)
                if has_next:
                    act.wait_ge(hlo_ready_pool, nxt.count(2, 0))
                if has_next:
                    u_copy(g, 0)
                    transposes(nxt, 4, 6)
                    t_copy(g, first)
                else:
                    t_copy(g, first)
                    u_copy(g, 0)
                if has_next:
                    transposes(nxt, 6, 7)
                u_copy(g, 1)
                if has_next:
                    transposes(nxt, 7, 8)
                if has_prev:
                    normalise(before, (0, 1))
                if not has_next:
                    exponent(g)
                u_copy(g, 2)
                if has_prev:
                    normalise(before, (2,))
                if has_next:
                    exponent(g)
                if has_prev:
                    normalise(before, (3,))
                u_copy(g, 3)

            for k in range(DC):
                act.wait_ge(gw_done, k + 1)
                if k:
                    act.activation(l_f32["lang"][:, blk(k, 0) * P:blk(k, k) * P], weight_bank[k][:, 0:k * P], ACT.Copy)
                act.activation(l_f32["lang"][:, blk(k, k) * P:(blk(k, k) + 1) * P],
                               weight_bank[k][:, k * P:(k + 1) * P], ACT.Copy, scale=0.5).then_inc(l_copied, 1)
            act.wait_ge(l_copied, DC)
            act.activation(square[0][:, 0:NBLK * P], l_f32["lang"][:, :], ACT.Square,
                           accum_out=ssq[:, 0:1]).then_inc(sq_summed, 1)
            for c in range(DC):
                act.wait_ge(wot_done, c + 1)
                act.activation(wo_t[:, c, :], front[c % 2][:, :], ACT.Copy).then_inc(wot_copied, 1)
            for p in range(PAIRS):
                h_high(Group(0, 0), p)
            act.wait_ge(small_loaded, 32)
            act.activation(gexp[:, :], gate_b[:, :], ACT.Exp, scale=-1.0).then_inc(act_const, 1)
            act.activation(sexp[:, :], lsig_b[:, :], ACT.Exp, scale=-2.0).then_inc(act_const, 1)
            act.wait_ge(hlo_ready, 4)
            transposes(Group(0, 0), 0, 3)
            act.wait_ge(g_copied, DC)
            act.activation(square[1][:, 0:NBLK * P], l_f32["grav"][:, :], ACT.Square,
                           accum_out=ssq[:, 1:2]).then_inc(sq_summed, 1)
            transposes(Group(0, 0), 3, 8)
            for s_n, s in enumerate(("lang", "grav")):
                act.wait_ge(scale_ready, 1)
                act.activation(l_hi[s][:, :, :].rearrange("p a b -> p (a b)"), l_f32[s][:, :], ACT.Copy,
                               scale=up[:, s_n:s_n + 1]).then_inc(wt_hi, 1)
            act.wait_ge(sq_summed, 2)
            for k in range(DC):
                act.wait_ge(m_copied, k + 1)
                act.activation(square[0][:, k * D:(k + 1) * D], m_f32[:, k, :], ACT.Square,
                               accum_out=ssq[:, 2 + k:3 + k]).then_inc(sq_summed, 1)
            act.wait_ge(sq_summed, 2 + DC)
            run(act, iteration, back)

        @block.vector
        def _(dve):
            def add_bias(g, p):
                dve.wait_ge(l0_done, g.count(4, p + 1))
                dve.tensor_tensor(y[:, p, :], front[p % 2][:, :], bias_b[:, :], ALU.add).then_inc(y_ready, 1)

            def row_stats(g, p):
                dve.wait_ge(y_ready, g.count(4, p + 1))
                dve.bn_stats(stats1[:, p, :], y[:, p, :]).then_inc(stats1_ready, 1)

            def row_moments(g):
                for p in range(PAIRS):
                    dve.bn_aggr(mv1[:, p, :], stats1[:, p, :]).then_inc(mv1_ready, 1)

            def norm_rows(g, readers=None):
                dve.wait_ge(rstd1_ready, g.count(1, 1))
                for p in range(PAIRS):
                    if readers:
                        dve.wait_ge(sum_ready, readers.count(4, p + 1))
                    dve.tensor_scalar(h[g.parity][:, p, :], y[:, p, :], mv1[:, p, 0:1], rstd1[:, p:p + 1],
                                      ALU.subtract, ALU.mult).then_inc(h_ready, 1)

            def h_low(g, p):
                dve.wait_ge(hhi_ready, g.count(4, p + 1))
                dve.tensor_tensor(h_lo[:, p, :], h[g.parity][:, p, :], h_hi[:, p, :],
                                  ALU.subtract).then_inc(hlo_ready, 1)

            def p_low(g, j):
                dve.wait_ge(phi_ready, g.count(8, j + 1))
                dve.tensor_tensor(p_lo[:, j % 4, :, j // 4, :], by_batch(proj[j % 3]),
                                  p_hi[:, j % 4, :, j // 4, :], ALU.subtract).then_inc(plo_ready, 1)

            def diagonals(g):
                dve.wait_ge(tdiag_ready, g.count(1, 1))
                dve.reduce_sum(diag[:, :], by_batch(t_diag), X_AXIS).then_inc(diag_ready, 1)
                dve.wait_ge(diag_ready, g.count(1, 1))
                dve.tensor_scalar(nsq[L, :], diag[L, :], 2.0, EPS_NORM_SQ, ALU.mult, ALU.max).then_inc(nsq_ready, 1)
                dve.tensor_scalar(vec[GR, :], diag[GR, :], 2.0, None, ALU.mult).then_inc(nsq_ready, 1)

            def diagonal_matrices(g):
                dve.wait_ge(rinv_ready, g.count(1, 1))
                dve.wait_ge(nsq_ready, g.count(2, 2))
                dve.tensor_tensor(by_batch(v_diag), over_batches(eye2), over_columns(vec),
                                  ALU.mult).then_inc(v_ready, 1)

            def sums(g):
                dve.wait_ge(sym_done, g.count(1, 1))
                dve.tensor_tensor(s_sb[:, :], ps_t[:, :], t_sb[:, :], ALU.add).then_inc(s_ready, 1)

            def distances(g):
                dve.wait_ge(dj_done, g.count(1, 1))
                dve.wait_ge(s_ready, g.count(1, 1))
                dve.scalar_tensor_tensor(out=s_sb[GR, :], in0=s_sb[GR, :], scalar=-2.0, in1=ps_v[GR, :],
                                         op0=ALU.mult, op1=ALU.add).then_inc(d2_ready, 1)
                dve.tensor_tensor(by_batch(w_sb, 0, N), by_batch(ps_v, 0, N), over_batches(mask, 0, N),
                                  ALU.mult).then_inc(mr_ready, 1)
                dve.wait_ge(d2_ready, g.count(2, 1))
                dve.tensor_tensor(by_batch(w_sb, N, P), by_batch(s_sb, N, P), over_columns(vec, N, P),
                                  ALU.add).then_inc(d2_ready, 1)

            def similarities(g):
                dve.wait_ge(mr_ready, g.count(1, 1))
                dve.scalar_tensor_tensor(out=a_sb[L, :], in0=s_sb[L, :], scalar=0.0, in1=w_sb[L, :],
                                         op0=ALU.max, op1=ALU.mult).then_inc(a_ready, 1)

            def gravities(g):
                dve.wait_ge(exp_ready, g.count(1, 1))
                dve.scalar_tensor_tensor(out=by_batch(a_sb, N, P), in0=by_batch(e_sb, N, P), scalar=1.0,
                                         in1=over_batches(mask, N, P), op0=ALU.min,
                                         op1=ALU.mult).then_inc(a_ready, 1)

            def row_factors(g, nxt):
                dve.wait_ge(a_ready, g.count(2, 2))
                dve.reduce_sum(deg[:, :], by_batch(a_sb), X_AXIS).then_inc(deg_ready, 1)
                if nxt:
                    row_stats(nxt, 0)
                dve.wait_ge(deg_ready, g.count(5, 1))
                dve.wait_ge(rr_ready, g.count(1, 1))
                dve.tensor_tensor(degr[:, :], deg[:, :], rr[:, :], ALU.mult).then_inc(deg_ready, 1)
                if nxt:
                    row_stats(nxt, 1)
                dve.wait_ge(deg_ready, g.count(5, 2))
                dve.tensor_scalar(degm[:, :], degr[:, :], EPS_DEG, None, ALU.max).then_inc(deg_ready, 1)
                dve.wait_ge(deg_ready, g.count(5, 3))
                dve.reciprocal(dinv[:, :], degm[:, :]).then_inc(deg_ready, 1)
                dve.wait_ge(deg_ready, g.count(5, 4))
                dve.scalar_tensor_tensor(out=cfac[:, :], in0=dinv[:, :], scalar=wv_scale[:, 0:1], in1=rr[:, :],
                                         op0=ALU.mult, op1=ALU.mult).then_inc(deg_ready, 1)

            def scale_rows(g):
                dve.wait_ge(deg_ready, g.count(5, 5))
                dve.tensor_tensor(by_batch(ks_sb), by_batch(a_sb), over_columns(cfac), ALU.mult).then_inc(ks_ready, 1)

            def residual(g, p, first):
                dve.wait_ge(ku_done, g.count(4, p + 1))
                if p == 0 and not first:
                    dve.wait_ge(o_moved, g.prev().count(16, 32))
                dve.tensor_tensor(o[:, p, :], ku_bank[p][:, :], h[g.parity][:, p, :], ALU.add).then_inc(sum_ready, 1)

            def out_stats(g, p):
                dve.wait_ge(sum_ready, g.count(4, p + 1))
                dve.bn_stats(stats2[:, p, :], o[:, p, :]).then_inc(stats2_ready, 1)

            def out_moments(g):
                dve.wait_ge(stats2_ready, g.count(4, 4))
                dve.tensor_scalar(hold[:, :], stats2[:, 0, 0:1], 1.0, None, ALU.mult)
                for p in range(PAIRS):
                    dve.bn_aggr(mv2[:, p, :], stats2[:, p, :]).then_inc(mv2_ready, 1)

            def out_shift(g):
                dve.wait_ge(rstd2_ready, g.count(1, 1))
                dve.scalar_tensor_tensor(out=nmr2[:, :], in0=mv2[:, :, 0], scalar=-1.0, in1=rstd2[:, :],
                                         op0=ALU.mult, op1=ALU.mult).then_inc(nmr2_ready, 1)

            def m_scale():
                dve.wait_ge(norm_done, 2)
                dve.tensor_scalar(ssq_all[:, 2:3], ps_k[:, 2:3], TINY, None, ALU.max).then_inc(norm_copied, 1)
                dve.wait_ge(norm_pow, 2)
                dve.tensor_scalar(up[:, 2:3], rnorm[:, 2:3], FP16_NORM, None, ALU.mult).then_inc(scale_ready, 1)
                dve.wait_ge(scale_ready, 3)
                dve.reciprocal(down[:, 2:3], up[:, 2:3]).then_inc(scale_ready, 1)
                dve.wait_ge(scale_ready, 4)
                dve.wait_ge(dve_const, 13)
                dve.tensor_tensor(wv_scale[:, :], wside[:, :], down[:, 2:3], ALU.mult).then_inc(scale_ready, 1)

            def m_low(k):
                dve.wait_ge(wt_hi, 3 + k // 2)
                dve.scalar_tensor_tensor(out=m_lo[:, k, :], in0=m_f32[:, k, :], scalar=up[:, 2:3],
                                         in1=m_hi[:, k, :], op0=ALU.mult, op1=ALU.subtract).then_inc(wt_lo, 1)

            def back(g):
                similarities(g)
                gravities(g)
                row_factors(g, None)
                scale_rows(g)
                def statistics(p):
                    dve.wait_ge(ku_done, g.count(4, p + 1))
                    dve.bn_stats(stats2[:, p, :], last_ku_bank[p][:, :]).then_inc(stats2_ready, 1)

                def moments(half):
                    dve.wait_ge(stats2_ready, g.count(4, 2 * half + 2))
                    dve.tensor_scalar(hold[:, :], stats2[:, 0, 0:1], 1.0, None, ALU.mult)
                    for p in (2 * half, 2 * half + 1):
                        dve.bn_aggr(mv2[:, p, :], stats2[:, p, :]).then_inc(mv2_ready, 1)

                def shift(half):
                    pairs = slice(2 * half, 2 * half + 2)
                    dve.wait_ge(rstd2_ready, g.count(1, 1 + half))
                    dve.scalar_tensor_tensor(out=nmr2[:, pairs], in0=mv2[:, pairs, 0], scalar=-1.0, in1=rstd2[:, pairs],
                                             op0=ALU.mult, op1=ALU.mult).then_inc(nmr2_ready, 1)

                statistics(0)
                statistics(1)
                moments(0)
                statistics(2)
                dve.wait_ge(o_moved, g.prev().count(16, 32))
                dve.wait_ge(ku_done, g.count(4, 4))
                dve.tensor_tensor(o[:, 3, :], last_ku_bank[3][:, :], h[g.parity][:, 3, :], ALU.add).then_inc(sum_ready, 1)
                shift(0)
                dve.wait_ge(sum_ready, g.count(4, 1))
                dve.bn_stats(stats2[:, 3, :], o[:, 3, :]).then_inc(stats2_ready, 1)
                moments(1)
                shift(1)
                dve.wait_ge(nmr2_ready, g.count(1, 2))
                dve.tensor_scalar(o[:, 3, :], o[:, 3, :], rstd2[:, 3:4], nmr2[:, 3:4],
                                  ALU.mult, ALU.add).then_inc(out_ready_dve, 1)

            def iteration(g, has_prev, has_next):
                first = not has_prev
                before = g.prev() if has_prev else None
                nxt = g.next() if has_next else None
                if has_prev:
                    similarities(before)
                    gravities(before)
                if has_next:
                    add_bias(nxt, 0)
                    add_bias(nxt, 1)
                if first:
                    m_scale()
                if has_prev:
                    row_factors(before, nxt)
                    p_low(g, 0)
                    scale_rows(before)
                else:
                    row_stats(nxt, 0)
                    row_stats(nxt, 1)
                    p_low(g, 0)
                    m_low(0)
                if has_next:
                    for p in (2, 3):
                        add_bias(nxt, p)
                    for p in (2, 3):
                        row_stats(nxt, p)
                    dve.wait_ge(stats1_ready, nxt.count(4, 4))
                p_low(g, 1)
                if has_next:
                    row_moments(nxt)
                if first:
                    m_low(1)
                if has_prev:
                    residual(before, 0, False)
                    residual(before, 1, False)
                    residual(before, 2, False)
                    residual(before, 3, False)
                p_low(g, 2)
                if has_next:
                    norm_rows(nxt, before)
                    h_low(nxt, 0)
                p_low(g, 3)
                if has_next:
                    h_low(nxt, 1)
                p_low(g, 4)
                if first:
                    m_low(2)
                p_low(g, 5)
                if first:
                    m_low(3)
                p_low(g, 6)
                p_low(g, 7)
                if has_prev:
                    for p in range(PAIRS):
                        out_stats(before, p)
                    out_moments(before)
                    out_shift(before)
                if not has_next:
                    dve.wait_ge(t_ready, g.count(1, 1))
                    dve.tensor_tensor(by_batch(t_diag), by_batch(t_sb), over_batches(eye2),
                                      ALU.mult).then_inc(tdiag_ready, 1)
                diagonals(g)
                diagonal_matrices(g)
                sums(g)
                distances(g)

            dve.memset(ones[:, :], 1.0).then_inc(dve_const, 1)
            dve.memset(minus_half[:, :], -0.5).then_inc(half_ready, 1)
            dve.wait_ge(adj_loaded, 32)
            dve.tensor_tensor(adj_sq[:, :], adj2[:, :], adj2[:, :], ALU.mult).then_inc(dve_const, 1)
            dve.wait_ge(dve_const, 2)
            dve.wait_ge(pool_const, 10)
            dve.tensor_tensor(wmix[L, L], adj_sq[L, :], eye2[L, :], ALU.add)
            dve.tensor_tensor(wmix[GR, GR], adj_sq[GR, :], eye2[GR, :], ALU.add).then_inc(dve_const, 1)
            dve.tensor_scalar(not_eye[:, :], eye2[:, :], -1.0, 1.0, ALU.mult, ALU.add).then_inc(dve_const, 1)
            dve.wait_ge(dve_const, 4)
            dve.tensor_tensor(mask[:, :], adj2[:, :], not_eye[:, :], ALU.mult).then_inc(dve_const, 1)
            dve.tensor_copy(eye_l[:, :], ident[:, 0:N]).then_inc(dve_const, 1)
            dve.tensor_copy(eye_g[:, :], ident[:, N:P]).then_inc(dve_const, 1)
            dve.memset(rr[:, :], 1.0).then_inc(dve_const, 1)
            g0 = Group(0, 0)
            dve.wait_ge(bias_loaded, 16)
            for p in range(PAIRS):
                add_bias(g0, p)
            for p in range(PAIRS):
                row_stats(g0, p)
            dve.wait_ge(stats1_ready, 4)
            row_moments(g0)
            norm_rows(g0)
            for p in range(PAIRS):
                h_low(g0, p)
            for k in range(DC):
                dve.wait_ge(gw_done, DC + k + 1)
                if k:
                    dve.tensor_copy(l_f32["grav"][:, blk(k, 0) * P:blk(k, k) * P], weight_bank[k][:, 0:k * P])
                dve.tensor_scalar(l_f32["grav"][:, blk(k, k) * P:(blk(k, k) + 1) * P],
                                  weight_bank[k][:, k * P:(k + 1) * P], 0.5, None, ALU.mult).then_inc(g_copied, 1)
            dve.wait_ge(act_const, 2)
            dve.tensor_scalar(gexp1[:, :], gexp[:, :], 1.0, None, ALU.add).then_inc(dve_const, 1)
            dve.tensor_scalar(cexp[:, :], sexp[:, :], -0.5, None, ALU.mult).then_inc(dve_const, 1)
            dve.wait_ge(dve_const, 10)
            dve.reciprocal(wgate[:, :], gexp1[:, :]).then_inc(dve_const, 1)
            dve.wait_ge(dve_const, 11)
            dve.tensor_copy(wside[L, :], wgate[L, :]).then_inc(dve_const, 1)
            dve.tensor_scalar(wside[GR, :], wgate[GR, :], -1.0, 1.0, ALU.mult, ALU.add).then_inc(dve_const, 1)
            def m_copy(k):
                dve.wait_ge(gw_done, 2 * DC + k + 1)
                dve.tensor_copy(m_f32[:, k, :], weight_bank[k][:, :]).then_inc(m_copied, 1)

            def weight_low(s_n):
                s = ("lang", "grav")[s_n]
                dve.wait_ge(wt_hi, s_n + 1)
                dve.scalar_tensor_tensor(out=l_lo[s][:, :, :].rearrange("p a b -> p (a b)"), in0=l_f32[s][:, :],
                                         scalar=up[:, s_n:s_n + 1],
                                         in1=l_hi[s][:, :, :].rearrange("p a b -> p (a b)"),
                                         op0=ALU.mult, op1=ALU.subtract).then_inc(wt_lo, 1)

            m_copy(0)
            dve.wait_ge(norm_done, 1)
            dve.tensor_scalar(ssq_all[:, 0:2], ps_k[:, 0:2], TINY, None, ALU.max).then_inc(norm_copied, 1)
            dve.wait_ge(norm_pow, 1)
            dve.tensor_scalar(up[:, 0:2], rnorm[:, 0:2], FP16_NORM, None, ALU.mult).then_inc(scale_ready, 1)
            dve.wait_ge(scale_ready, 1)
            dve.reciprocal(down[:, 0:2], up[:, 0:2]).then_inc(scale_ready, 1)
            dve.wait_ge(scale_ready, 2)
            dve.tensor_copy(t_scale[L, :], down[L, 0:1]).then_inc(t_scale_ready, 1)
            dve.tensor_copy(t_scale[GR, :], down[GR, 1:2]).then_inc(t_scale_ready, 1)
            m_copy(1)
            weight_low(0)
            weight_low(1)
            m_copy(2)
            m_copy(3)
            run(dve, iteration, back)

        @block.gpsimd
        def _(pool):
            def inverse_std(g, mv_ready, mv, ve_ready, ve, rstd_ready, rstd):
                pool.wait_ge(mv_ready, g.count(4, 4))
                pool.tensor_tensor(ve[:, :], mv[:, :, 1], eps_ln[:, :], ALU.add).then_inc(ve_ready, 1)
                pool.wait_ge(ve_ready, g.count(1, 1))
                pool.tensor_tensor(rstd[:, :], ve[:, :], minus_half[:, 0:PAIRS], ALU.pow).then_inc(rstd_ready, 1)

            def ln1(g):
                inverse_std(g, mv1_ready, mv1, ve1_ready, ve1, rstd1_ready, rstd1)

            def ln2(g):
                inverse_std(g, mv2_ready, mv2, ve2_ready, ve2, rstd2_ready, rstd2)

            def last_ln2(g):
                for half in range(2):
                    pairs = slice(2 * half, 2 * half + 2)
                    pool.wait_ge(mv2_ready, g.count(4, 2 * half + 2))
                    pool.tensor_tensor(ve2[:, pairs], mv2[:, pairs, 1], eps_ln[:, pairs], ALU.add).then_inc(ve2_ready, 1)
                    pool.wait_ge(ve2_ready, g.count(1, 1 + half))
                    pool.tensor_tensor(rstd2[:, pairs], ve2[:, pairs], minus_half[:, pairs],
                                       ALU.pow).then_inc(rstd2_ready, 1)

            def t_diagonal(g):
                pool.wait_ge(t_ready, g.count(1, 1))
                pool.tensor_tensor(by_batch(t_diag), by_batch(t_sb), over_batches(eye2),
                                   ALU.mult).then_inc(tdiag_ready, 1)

            def inverse_norm(g):
                pool.wait_ge(nsq_ready, g.count(2, 1))
                pool.tensor_tensor(vec[L, :], nsq[L, :], minus_half[L, :], ALU.pow).then_inc(rinv_ready, 1)
                pool.tensor_tensor(rr[L, :], nsq[L, :], minus_half[L, :], ALU.pow).then_inc(rr_ready, 1)

            def iteration(g, has_prev, has_next):
                if not has_prev:
                    pool.wait_ge(norm_copied, 2)
                    pool.tensor_tensor(rnorm[:, 2:3], ssq_all[:, 2:3], minus_half[:, 2:3], ALU.pow).then_inc(norm_pow, 1)
                if has_next:
                    ln1(g.next())
                    for p in (2, 3):
                        pool.wait_ge(hhi_ready, g.next().count(4, p + 1))
                        pool.tensor_tensor(h_lo[:, p, :], h[g.next().parity][:, p, :], h_hi[:, p, :],
                                           ALU.subtract).then_inc(hlo_ready_pool, 1)
                if has_prev:
                    ln2(g.prev())
                if has_next:
                    t_diagonal(g)
                inverse_norm(g)

            pool.memset(ident[:, :], 0.0).then_inc(pool_const, 1)
            pool.wait_ge(pool_const, 1)
            pool.affine_select(out=ident[:, :], in_=ident[:, :], compare_op=ALU.not_equal, fill=1.0, base=0,
                               pattern=[[-1, P]], channel_multiplier=1).then_inc(pool_const, 1)
            pool.wait_ge(pool_const, 2)
            pool.tensor_copy(eye2[L, :], ident[L, 0:N]).then_inc(pool_const, 1)
            pool.wait_ge(pool_const, 3)
            pool.tensor_copy(eye2[GR, :], ident[GR, N:P]).then_inc(pool_const, 1)
            pool.wait_ge(pool_const, 4)
            pool.memset(ones_lg[:, :], 0.0).then_inc(pool_const, 1)
            pool.wait_ge(pool_const, 5)
            pool.memset(ones_lg[L, 0:N], 1.0).then_inc(pool_const, 1)
            pool.wait_ge(pool_const, 6)
            pool.memset(ones_lg[GR, N:P], 1.0).then_inc(pool_const, 1)
            pool.wait_ge(pool_const, 7)
            pool.memset(kt[:, :, :], 0.0).then_inc(pool_const, 1)
            pool.memset(eps_ln[:, :], EPS_LN).then_inc(pool_const, 1)
            pool.memset(wmix[:, :], 0.0).then_inc(pool_const, 1)
            pool.wait_ge(pool_const, 10)
            pool.wait_ge(half_ready, 1)
            ln1(Group(0, 0))
            pool.wait_ge(norm_copied, 1)
            pool.tensor_tensor(rnorm[:, 0:2], ssq_all[:, 0:2], minus_half[:, 0:2], ALU.pow).then_inc(norm_pow, 1)
            run(pool, iteration, last_ln2)


_INS = ["x", "adj", "L0_gnn_bias", "L1_gnn_W_lang", "L1_gnn_W_grav", "L1_gnn_W_V", "L1_gnn_W_O",
        "L1_gnn_gate_logit", "L1_gnn_log_sigma"]


def kernel(**inputs):
    import numpy as np
    import concourse.bacc as bacc
    from concourse.bass_utils import run_bass_kernel_spmd

    nc = bacc.Bacc("TRN2", target_bir_lowering=False, num_devices=1)
    arrays, args = {}, []
    for name in _INS:
        a = np.ascontiguousarray(inputs[name])
        arrays[f"in_{name}"] = a
        args.append(nc.dram_tensor(f"in_{name}", a.shape, mybir.dt.from_np(a.dtype), kind="ExternalInput").ap())
    shape = inputs["x"].shape
    out = nc.dram_tensor("out", shape, F32, kind="ExternalOutput").ap()
    resnorm_graph_kernel(nc, *args, out)
    r = run_bass_kernel_spmd(nc, [arrays], core_ids=[0])
    return r.results[0]["out"]
```
